# Optimizing a Trainium2 kernel written in Bass

```python
import numpy as np
import jax
import jax.numpy as jnp

def _softmax(x, axis=-1):
    return jax.nn.softmax(x, axis=axis)

def _gelu(x):
    return jax.nn.gelu(x, approximate=True)

def _silu(x):
    return jax.nn.silu(x)

def _sigmoid(x):
    return jax.nn.sigmoid(x)

def _layernorm(x, axis=-1, eps=1e-05):
    m = jnp.mean(x, axis=axis, keepdims=True)
    v = jnp.var(x, axis=axis, keepdims=True)
    return (x - m) / jnp.sqrt(v + eps)

def _scatter_add(tgt, idx, src, axis=0):
    return tgt.at[idx].add(src)

def _segment_sum(src, seg, n):
    return jax.ops.segment_sum(src, seg, n)
kernel_name = 'mk_sandwich_d2_jaxref_r8_0d619f'

def setup_inputs(seed: int=0):
    np.random.seed(seed)
    _w = jnp.asarray

    def _L0_attn_setup():
        import jax, jax.numpy as jnp
        import numpy as np
        B, T, D = (4, 256, 128)
        NUM_HEADS, HEAD_DIM = (16, 64)
        ROPE_THETA = 10000.0

        def precompute_freqs_cis(dim, max_seq_len, theta=10000.0):
            inv_freq = 1.0 / theta ** (jnp.arange(0, dim, 2, dtype=jnp.float32) / dim)
            freqs = jnp.outer(jnp.arange(max_seq_len, dtype=jnp.float32), inv_freq)
            return (jnp.cos(freqs), jnp.sin(freqs))

        def apply_rotary_emb(x, cos, sin):
            c = cos[None, None, :, :]
            s = sin[None, None, :, :]
            x1, x2 = jnp.split(x.astype(jnp.float32), 2, axis=-1)
            return jnp.concatenate([x1 * c - x2 * s, x1 * s + x2 * c], axis=-1).astype(x.dtype)
        key = jax.random.key(seed)
        ks = jax.random.split(key, 5)
        scale = 1.0 / np.sqrt(D)
        return {'x': jax.random.normal(ks[0], (B, T, D), dtype=jnp.float32), 'wq': jax.random.normal(ks[1], (NUM_HEADS * HEAD_DIM, D), dtype=jnp.float32) * scale, 'wk': jax.random.normal(ks[2], (NUM_HEADS * HEAD_DIM, D), dtype=jnp.float32) * scale, 'wv': jax.random.normal(ks[3], (NUM_HEADS * HEAD_DIM, D), dtype=jnp.float32) * scale, 'wo': jax.random.normal(ks[4], (D, NUM_HEADS * HEAD_DIM), dtype=jnp.float32) * scale}
    _L0_attn_in = _L0_attn_setup()

    def _L0_ffn_setup():
        import jax, jax.numpy as jnp
        import numpy as np
        DIM = 128
        HIDDEN = 384
        SCALE = 1.0 / 127.0

        def _dequant(w_int, dtype):
            return w_int.astype(dtype) * jnp.asarray(SCALE, dtype)
        key = jax.random.key(seed)
        k_x, k_g, k_u, k_d = jax.random.split(key, 4)
        x = jax.random.normal(k_x, (4, 256, DIM), dtype=jnp.float32)
        w_gate = jax.random.randint(k_g, (HIDDEN, DIM), -127, 128, dtype=jnp.int32)
        w_up = jax.random.randint(k_u, (HIDDEN, DIM), -127, 128, dtype=jnp.int32)
        w_down = jax.random.randint(k_d, (DIM, HIDDEN), -127, 128, dtype=jnp.int32)
        return {'x': x, 'w_gate': w_gate, 'w_up': w_up, 'w_down': w_down}
    _L0_ffn_in = _L0_ffn_setup()

    def _L1_attn_setup():
        import jax, jax.numpy as jnp
        import numpy as np
        B, L, D, H = (2, 256, 128, 16)
        C = D // H
        SCALE = 1.0 / np.sqrt(D).astype(np.float32)
        key = jax.random.key(seed)
        ks = jax.random.split(key, 5)
        return {'x': jax.random.normal(ks[0], (B, L, D), dtype=jnp.float32), 'w_qkv': jax.random.normal(ks[1], (3 * D, D), dtype=jnp.float32) * (1.0 / np.sqrt(D)), 'b_qkv': jax.random.normal(ks[2], (3 * D,), dtype=jnp.float32) * 0.02, 'w_o': jax.random.normal(ks[3], (D, D), dtype=jnp.float32) * (1.0 / np.sqrt(D)), 'b_o': jax.random.normal(ks[4], (D,), dtype=jnp.float32) * 0.02}
    _L1_attn_in = _L1_attn_setup()

    def _L1_ffn_setup():
        import jax, jax.numpy as jnp
        import numpy as np
        S, B, D, H, E, K, F = (128, 4, 128, 16, 8, 2, 512)

        def _ln(x, g, b, eps=1e-05):
            mu = jnp.mean(x, axis=-1, keepdims=True)
            var = jnp.mean((x - mu) ** 2, axis=-1, keepdims=True)
            return (x - mu) * jax.lax.rsqrt(var + eps) * g + b
        key = jax.random.key(seed)
        ks = jax.random.split(key, 8)
        s = 0.02
        return {'src': jax.random.normal(ks[0], (S, B, D), jnp.float32), 'in_proj_w': jax.random.normal(ks[1], (3 * D, D), jnp.float32) * s, 'in_proj_b': jnp.zeros((3 * D,), jnp.float32), 'out_w': jax.random.normal(ks[2], (D, D), jnp.float32) * s, 'out_b': jnp.zeros((D,), jnp.float32), 'gate_w': jax.random.normal(ks[3], (E, D), jnp.float32) * s, 'gate_b': jnp.zeros((E,), jnp.float32), 'w1': jax.random.normal(ks[4], (E, F, D), jnp.float32) * s, 'b1': jnp.zeros((E, F), jnp.float32), 'w2': jax.random.normal(ks[5], (E, D, F), jnp.float32) * s, 'b2': jnp.zeros((E, D), jnp.float32), 'ln1_g': jnp.ones((D,), jnp.float32), 'ln1_b': jnp.zeros((D,), jnp.float32), 'ln2_g': jnp.ones((D,), jnp.float32), 'ln2_b': jnp.zeros((D,), jnp.float32)}
    _L1_ffn_in = _L1_ffn_setup()
    _d = {'L0_attn_x': _L0_attn_in['x'], 'L0_attn_wq': _L0_attn_in['wq'], 'L0_attn_wk': _L0_attn_in['wk'], 'L0_attn_wv': _L0_attn_in['wv'], 'L0_attn_wo': _L0_attn_in['wo'], 'L0_ffn_w_gate': _L0_ffn_in['w_gate'], 'L0_ffn_w_up': _L0_ffn_in['w_up'], 'L0_ffn_w_down': _L0_ffn_in['w_down'], 'L1_attn_w_qkv': _L1_attn_in['w_qkv'], 'L1_attn_b_qkv': _L1_attn_in['b_qkv'], 'L1_attn_w_o': _L1_attn_in['w_o'], 'L1_attn_b_o': _L1_attn_in['b_o'], 'L1_ffn_in_proj_w': _L1_ffn_in['in_proj_w'], 'L1_ffn_in_proj_b': _L1_ffn_in['in_proj_b'], 'L1_ffn_out_w': _L1_ffn_in['out_w'], 'L1_ffn_out_b': _L1_ffn_in['out_b'], 'L1_ffn_gate_w': _L1_ffn_in['gate_w'], 'L1_ffn_gate_b': _L1_ffn_in['gate_b'], 'L1_ffn_w1': _L1_ffn_in['w1'], 'L1_ffn_b1': _L1_ffn_in['b1'], 'L1_ffn_w2': _L1_ffn_in['w2'], 'L1_ffn_b2': _L1_ffn_in['b2'], 'L1_ffn_ln1_g': _L1_ffn_in['ln1_g'], 'L1_ffn_ln1_b': _L1_ffn_in['ln1_b'], 'L1_ffn_ln2_g': _L1_ffn_in['ln2_g'], 'L1_ffn_ln2_b': _L1_ffn_in['ln2_b']}
    _x0 = _d['L0_attn_x']
    _d['L0_attn_x'] = jax.random.normal(jax.random.fold_in(jax.random.key(seed), 1), (4, 1024, 128), dtype=_x0.dtype)
    del _x0
    return _d

def reference(L0_attn_x, L0_attn_wq, L0_attn_wk, L0_attn_wv, L0_attn_wo, L0_ffn_w_gate, L0_ffn_w_up, L0_ffn_w_down, L1_attn_w_qkv, L1_attn_b_qkv, L1_attn_w_o, L1_attn_b_o, L1_ffn_in_proj_w, L1_ffn_in_proj_b, L1_ffn_out_w, L1_ffn_out_b, L1_ffn_gate_w, L1_ffn_gate_b, L1_ffn_w1, L1_ffn_b1, L1_ffn_w2, L1_ffn_b2, L1_ffn_ln1_g, L1_ffn_ln1_b, L1_ffn_ln2_g, L1_ffn_ln2_b):

    def _L0_attn_ref(x, wq, wk, wv, wo):
        import jax, jax.numpy as jnp
        import numpy as np
        B, T, D = (4, 256, 128)
        NUM_HEADS, HEAD_DIM = (16, 64)
        ROPE_THETA = 10000.0

        def precompute_freqs_cis(dim, max_seq_len, theta=10000.0):
            inv_freq = 1.0 / theta ** (jnp.arange(0, dim, 2, dtype=jnp.float32) / dim)
            freqs = jnp.outer(jnp.arange(max_seq_len, dtype=jnp.float32), inv_freq)
            return (jnp.cos(freqs), jnp.sin(freqs))

        def apply_rotary_emb(x, cos, sin):
            c = cos[None, None, :, :]
            s = sin[None, None, :, :]
            x1, x2 = jnp.split(x.astype(jnp.float32), 2, axis=-1)
            return jnp.concatenate([x1 * c - x2 * s, x1 * s + x2 * c], axis=-1).astype(x.dtype)
        batch, seq_len, _ = x.shape
        q = jnp.einsum('btd,od->bto', x, wq, preferred_element_type=jnp.float32)
        k = jnp.einsum('btd,od->bto', x, wk, preferred_element_type=jnp.float32)
        v = jnp.einsum('btd,od->bto', x, wv, preferred_element_type=jnp.float32)
        q = q.reshape(batch, seq_len, NUM_HEADS, HEAD_DIM).transpose(0, 2, 1, 3)
        k = k.reshape(batch, seq_len, NUM_HEADS, HEAD_DIM).transpose(0, 2, 1, 3)
        v = v.reshape(batch, seq_len, NUM_HEADS, HEAD_DIM).transpose(0, 2, 1, 3)
        cos, sin = precompute_freqs_cis(HEAD_DIM, seq_len, ROPE_THETA)
        q = apply_rotary_emb(q, cos, sin)
        k = apply_rotary_emb(k, cos, sin)
        scale = jnp.asarray(HEAD_DIM ** (-0.5), dtype=jnp.float32)
        scores = jnp.einsum('bhid,bhjd->bhij', q, k, preferred_element_type=jnp.float32) * scale
        causal = jnp.tril(jnp.ones((seq_len, seq_len), dtype=bool))
        scores = jnp.where(causal, scores, -jnp.inf)
        probs = jax.nn.softmax(scores, axis=-1).astype(x.dtype)
        out = jnp.einsum('bhij,bhjd->bhid', probs, v, preferred_element_type=jnp.float32).astype(x.dtype)
        out = out.transpose(0, 2, 1, 3).reshape(batch, seq_len, NUM_HEADS * HEAD_DIM)
        out = jnp.einsum('btd,od->bto', out, wo, preferred_element_type=jnp.float32)
        return out

    def _L0_ffn_ref(x, w_gate, w_up, w_down):
        import jax, jax.numpy as jnp
        import numpy as np
        DIM = 128
        HIDDEN = 384
        SCALE = 1.0 / 127.0

        def _dequant(w_int, dtype):
            return w_int.astype(dtype) * jnp.asarray(SCALE, dtype)
        wg = _dequant(w_gate, x.dtype)
        wu = _dequant(w_up, x.dtype)
        wd = _dequant(w_down, x.dtype)
        gate = jnp.einsum('bsd,hd->bsh', x, wg)
        up = jnp.einsum('bsd,hd->bsh', x, wu)
        h = jax.nn.silu(gate) * up
        return jnp.einsum('bsh,dh->bsd', h, wd)

    def _L1_attn_ref(x, w_qkv, b_qkv, w_o, b_o):
        import jax, jax.numpy as jnp
        import numpy as np
        B, L, D, H = (2, 256, 128, 16)
        C = D // H
        SCALE = 1.0 / np.sqrt(D).astype(np.float32)
        b, l, d = x.shape
        h, c = (H, d // H)
        qkv = jnp.einsum('bld,ed->ble', x, w_qkv) + b_qkv
        q, k, v = jnp.split(qkv, 3, axis=-1)
        q = q.reshape(b, l, h, c)
        k = k.reshape(b, l, h, c)
        v = v.reshape(b, l, h, c)
        attn = jax.nn.softmax(jnp.einsum('blhc,bmhc->bhlm', q, k) * SCALE, axis=-1)
        heads = jnp.einsum('bhlm,bmhc->blhc', attn, v).reshape(b, l, d)
        return jnp.einsum('bld,ed->ble', heads, w_o) + b_o + x

    def _L1_ffn_ref(src, in_proj_w, in_proj_b, out_w, out_b, gate_w, gate_b, w1, b1, w2, b2, ln1_g, ln1_b, ln2_g, ln2_b):
        import jax, jax.numpy as jnp
        import numpy as np
        S, B, D, H, E, K, F = (128, 4, 128, 16, 8, 2, 512)

        def _ln(x, g, b, eps=1e-05):
            mu = jnp.mean(x, axis=-1, keepdims=True)
            var = jnp.mean((x - mu) ** 2, axis=-1, keepdims=True)
            return (x - mu) * jax.lax.rsqrt(var + eps) * g + b
        s_len, bsz, d = src.shape
        dh = d // H
        qkv = src @ in_proj_w.T + in_proj_b
        q, k, v = jnp.split(qkv, 3, axis=-1)
        q = q.reshape(s_len, bsz, H, dh)
        k = k.reshape(s_len, bsz, H, dh)
        v = v.reshape(s_len, bsz, H, dh)
        scale = dh ** (-0.5)
        scores = jnp.einsum('sbhd,tbhd->bhst', q, k) * scale
        attn = jax.nn.softmax(scores, axis=-1)
        ctx = jnp.einsum('bhst,tbhd->sbhd', attn, v).reshape(s_len, bsz, d)
        attn_out = ctx @ out_w.T + out_b
        x = _ln(src + attn_out, ln1_g, ln1_b)
        tok = x.reshape(-1, d)
        n_tok = tok.shape[0]
        logits = tok @ gate_w.T + gate_b
        probs = jax.nn.softmax(logits, axis=-1)
        topv, topi = jax.lax.top_k(probs, K)
        topv = topv / jnp.sum(topv, axis=-1, keepdims=True)
        combine = jnp.zeros_like(probs).at[jnp.arange(n_tok)[:, None], topi].set(topv)
        moe_out = jnp.zeros_like(tok)
        for e in range(E):
            h = jax.nn.relu(tok @ w1[e].T + b1[e]) @ w2[e].T + b2[e]
            moe_out = moe_out + combine[:, e:e + 1] * h
        moe_out = moe_out.reshape(s_len, bsz, d)
        return _ln(x + moe_out, ln2_g, ln2_b)
    x = L0_attn_x
    x = x + _layernorm(_L0_attn_ref(_layernorm(x, axis=-1), L0_attn_wq, L0_attn_wk, L0_attn_wv, L0_attn_wo), axis=-1)
    x = x + _layernorm(_L0_ffn_ref(_layernorm(x, axis=-1), L0_ffn_w_gate, L0_ffn_w_up, L0_ffn_w_down), axis=-1)
    x = x + _layernorm(_L1_attn_ref(_layernorm(x, axis=-1), L1_attn_w_qkv, L1_attn_b_qkv, L1_attn_w_o, L1_attn_b_o), axis=-1)
    x = x + _layernorm(_L1_ffn_ref(_layernorm(x, axis=-1), L1_ffn_in_proj_w, L1_ffn_in_proj_b, L1_ffn_out_w, L1_ffn_out_b, L1_ffn_gate_w, L1_ffn_gate_b, L1_ffn_w1, L1_ffn_b1, L1_ffn_w2, L1_ffn_b2, L1_ffn_ln1_g, L1_ffn_ln1_b, L1_ffn_ln2_g, L1_ffn_ln2_b), axis=-1)
    return x

_drawn_inputs = setup_inputs


def setup_inputs(seed=0):
    import zlib

    import numpy as np

    out = dict(_drawn_inputs(seed))
    spreads = {'L1_ffn_in_proj_b': (0.0, 0.8),
     'L1_ffn_out_b': (0.0, 0.275),
     'L1_ffn_gate_b': (0.0, 0.554),
     'L1_ffn_b1': (0.0, 0.8),
     'L1_ffn_b2': (0.0, 0.414),
     'L1_ffn_ln1_g': (1.0, 0.2),
     'L1_ffn_ln1_b': (0.0, 0.285),
     'L1_ffn_ln2_g': (1.0, 0.2),
     'L1_ffn_ln2_b': (0.0, 0.282)}
    factors = {'L1_attn_b_qkv': 6.833,
     'L1_attn_b_o': 7.364,
     'L1_ffn_in_proj_w': 7.283,
     'L1_ffn_out_w': 5.381,
     'L1_ffn_w1': 4.846,
     'L1_ffn_w2': 3.789}
    for name, (base, spread) in spreads.items():
        noise = np.random.default_rng([zlib.crc32(name.encode()), seed]).standard_normal(out[name].shape)
        drawn = base * np.exp(spread * noise) if base else spread * noise
        out[name] = jnp.asarray(drawn.astype(out[name].dtype))
    for name, factor in factors.items():
        out[name] = (out[name] * factor).astype(out[name].dtype)
    return out
```

```python
from contextlib import ExitStack, contextmanager

import concourse.bass as bass
from concourse import mybir

F32 = mybir.dt.float32
F32R = mybir.dt.float32r
I32 = mybir.dt.int32
ACT = mybir.ActivationFunctionType
ALU = mybir.AluOpType
AX = mybir.AxisListType

P = 128
B, T, D = 4, 1024, 128
TILES = T // P
CH = 512
H0, C0 = 16, 64
PAIRS = H0 // 2
FFN = 384
FT = FFN // P
H1, C1 = 16, 8
GROUPS, GH = 4, 4
EXPERTS, HID = 8, 512
EPS = 1e-5
SCALE0 = C0 ** -0.5
SCALE1 = D ** -0.5
SCALE2 = C1 ** -0.5
MASKED = -1e30

PACK = [
    ("wqk1", 2 * GROUPS * P), ("ident", P), ("mask_st", P), ("mask_qk", P), ("wo0", PAIRS * D), ("wv1", D), ("wo1", D),
    ("win", 3 * D), ("wout", D), ("wgate", EXPERTS), ("bv1", D), ("bo1", D), ("bin", 3 * D), ("bout", D),
    ("bgate", EXPERTS), ("ln1g", D), ("ln1b", D), ("ln2g", D), ("ln2b", D), ("rank", EXPERTS),
    ("qb", 1), ("qc", 1), ("kb", 1), ("kc", 1), ("ke", 1), ("bias1", 2 * GROUPS), ("b2", D),
]
WL0 = 5 * P
WE = HID + HID // P * D + HID // P

PER = {
    "batch": {
        "av1_free": 4, "av_free": 32, "av_full": 36, "batch_done": 1, "dve_own": 82, "hi1_done": 8,
        "hi_done": 64, "klo_done": 16, "ms_act": 38, "ms_dve": 488, "ms_free": 471, "outT_ready": 1,
        "p_ready": 256, "p_used": 140, "pool_own": 17, "pool_prep": 2, "qlo_done": 16, "rope_done": 32,
        "rows0_loaded": 256, "rows1_loaded": 256, "rows_ready": 12, "rstd_ready": 6, "sg_ready": 6,
        "st_full": 256, "stack_done": 20, "var_ready": 6, "w0_loaded": 128, "xb_loaded": 16,
        "xn_ready": 3,
    },
    "pairs": {
        "av_free": 8, "av_full": 8, "dve_own": 14, "hi_done": 16, "klo_done": 4, "ms_act": 4,
        "ms_dve": 56, "ms_free": 50, "p_ready": 32, "p_used": 28, "qlo_done": 4, "rope_done": 8,
        "rows0_loaded": 64, "rows_ready": 2, "st_full": 32, "w0_loaded": 32,
    },
    "tokens": {
        "dve_own": 39, "ex_ready": 2, "ms_act": 4, "ms_dve": 5, "ms_free": 5, "rstd_ready": 2,
        "sc_ready": 2, "tok_ready": 2, "var_ready": 2, "xn_ready": 2,
    },
    "experts": {
        "h_full": 64, "relu_done": 64, "we0_loaded": 16, "we1_loaded": 16, "y_full": 16, "y_used": 16,
    },
    "chunks": {
        "h_full": 8, "relu_done": 8, "y_full": 2, "y_used": 2,
    },
    "last": {
        "dve_own": 18, "o_ready": 2, "rstd_ready": 4, "stored0": 16, "stored1": 16, "var_ready": 4,
    },
}


class Tally:

    def __init__(self, name, sem, start=0, step=1):
        self.name, self.sem, self.turn, self.n, self.step, self.total = name, sem, start, 0, step, 0

    def value(self):
        return self.turn + self.n

    def count(self, k=1):
        self.n += k * self.step
        self.total += k * self.step

    def up(self):
        self.count()
        return self.step

    def next(self, k=1):
        self.count(k)
        return self.value()

    def seen(self, more=0):
        return self.value() + more


class Signal:

    def __init__(self, sem, step):
        self.sem, self.step = sem, step

    def up(self):
        return self.step


@contextmanager
def repeat(engine, name, count, tallies):
    before = [(t, t.value(), t.total) for t in tallies]
    per = PER[name]
    with engine.Fori(0, count) as i:
        for t in tallies:
            t.turn, t.n, t.total = t.value() + i * per.get(t.name, 0) if per.get(t.name, 0) else t.value(), 0, 0
        yield i
        for t in tallies:
            assert t.total == per.get(t.name, 0), (name, t.name, t.total)
    for t, value, total in before:
        t.turn, t.n, t.total = value + count * per.get(t.name, 0), 0, total + count * per.get(t.name, 0)


def block_program(nc, x_in, pack, rope, wl0, wffn, wmoe, out):
    with ExitStack() as ctx:
        def sb(name, shape, dt=F32):
            return ctx.enter_context(nc.sbuf_tensor(name, shape, dt))

        sems = {}

        def sem(name):
            sems[name] = ctx.enter_context(nc.semaphore(name))

        x_all = sb("x_all", [P, B * TILES, D])
        cst = sb("cst", [P, sum(w for _, w in PACK)])
        at = {}
        col = 0
        for name, w in PACK:
            at[name] = cst[:, col:col + w]
            col += w
        ident_r = sb("ident_r", [P, P], F32R)
        mask_st = sb("mask_st_r", [P, P], F32R)
        mask_qk = sb("mask_qk_r", [P, P], F32R)
        wf = sb("wf", [P, 3 * FT, D])
        w0 = sb("w0", [P, 5, P])
        neghalf = sb("neghalf", [P, 1])
        stats = sb("stats", [P, TILES, 6])
        mv = sb("mv", [P, TILES, 2])
        var = sb("var", [P, TILES])
        rstd = sb("rstd", [P, TILES])
        mx = sb("mx", [P, 2, GH * TILES])
        mrows = sb("mrows", [GH * TILES, P], F32R)
        xb = sb("xb", [P, TILES, D])
        xn = sb("xn", [P, TILES, D])
        xT = sb("xT", [P, T])
        y = sb("y", [P, TILES, D])

        parts = sb("parts", [P, 16, T], F32R)
        ops0 = parts[:].rearrange("p (u k h) t -> p u k h t", u=2, k=4)
        QA, QB, KA, KB = 0, 1, 2, 3
        ops1 = parts[:, 0:10].rearrange("p (u k) t -> p u k t", u=2)

        big = sb("big", [P, 8, T])
        outT = big
        hT = big
        p1 = big[:].rearrange("p (u g) t -> p u g t", u=2)
        x1 = big[:, 0:4].rearrange("p a (n d) -> p (a n) d", d=D)
        x1T = big[:, 4:8].rearrange("p a t -> p (a t)")

        vals = sb("vals", [P, 4, T])
        v0 = vals[:].rearrange("p (u k) (t c) -> p u (k t) c", u=2, c=2 * P)
        v0 = v0.rearrange("p u t (h c) -> p u t h c", h=2)
        v1 = vals[:].rearrange("p k (t h c) -> p (k t) h c", t=2, c=32)
        acc = vals[:].rearrange("p a (n d) -> p (a n) d", d=D)

        p0 = sb("p0", [P, 2, T])
        tabs = sb("tabs", [P, 2 * WE])
        cosT, sinT = tabs[:, 0:T], tabs[:, T:2 * T]
        we = tabs[:].rearrange("p (u w) -> p u w", u=2)

        scr = sb("scr", [P, 5, T])
        qs, ks = scr[:, 0], scr[:, 1]
        t1, t2 = scr[:, 2, 0:CH], scr[:, 2, CH:T]
        sums = scr[:, 3:5]
        xq, xk, hq, hk = scr[:, 0], scr[:, 1], scr[:, 2], scr[:, 3]
        tqk = scr[:, 4]
        wfi = scr[:, 0:2].rearrange("p a t -> p (a t)")[:, 0:3 * FT * D].bitcast(I32)
        sg = scr[:, 0, 0:CH]
        relu = scr[:, 0:4].rearrange("p (u k) (f t) -> p u (k f) t", u=2, f=2)
        qkv = scr[:, 0:2].rearrange("p a t -> p (a t)")[:, 0:B * 3 * D].rearrange("p (s c) -> p s c", s=B)
        flat = scr[:, 2:4].rearrange("p a t -> p (a t)")
        prod = scr[:, 2:4].rearrange("p a (b t c) -> p (a b) t c", b=2, c=D)
        sc = scr[:, 4, 0:256].rearrange("p (s t h) -> p s t h", s=B, t=B)
        ex = scr[:, 4, 256:512].rearrange("p (s t h) -> p s t h", s=B, t=B)
        m2 = scr[:, 4, 512:576].rearrange("p (s h) -> p s h", s=B)
        sm2 = scr[:, 4, 576:640].rearrange("p (s h) -> p s h", s=B)
        gt = [scr[:, 4, 640 + 32 * k:672 + 32 * k].rearrange("p (s e) -> p s e", s=B) for k in range(8)]
        gm = [scr[:, 4, 896 + 4 * k:900 + 4 * k] for k in range(8)]
        cT, cbT = p0[:, 0, 0:CH], p0[:, 0, CH:T]
        sT = p0[:, 1, 0:CH]
        xs = x_all[:].rearrange("p (s i) d -> p s i d", s=B)
        ocur = p0[:, :, 0:CH].rearrange("p u (s d) -> p u s d", s=B)
        rinv = stats[:].rearrange("p i s -> p (i s)")[:, 0:TILES * GH].rearrange("p (i g) -> p i g", g=GH)
        bias_whole = tabs[:, 2 * T:2 * T + 2 * GROUPS]
        bias_high = sb("bias_high", [P, 2 * GROUPS])
        comb = xb[:, 0:2, :].rearrange("p a (n e) -> p (a n) e", e=EXPERTS)

        st = ctx.enter_context(nc.psum_tensor("st", [P, 2, T], F32))
        av = ctx.enter_context(nc.psum_tensor("av", [P, T], F32))
        ms = ctx.enter_context(nc.psum_tensor("ms", [P, T], F32))
        ms3 = ms[:].rearrange("p (n d) -> p n d", d=D)

        for name in (
            "loaded", "xb_loaded", "w0_loaded", "rows0_loaded", "rows1_loaded", "we0_loaded", "we1_loaded", "stored0",
            "stored1",
            "dve_own", "act_own", "pool_own",
            "prep_done", "pool_prep",
            "var_ready", "rstd_ready", "xn_ready",
            "ms_dve", "ms_act", "ms_free",
            "st_full", "p_ready", "p_used",
            "av_full", "av_free", "av1_free",
            "rope_done", "hi_done", "qlo_done", "klo_done", "rows_ready", "apart", "outT_ready",
            "hi1_done", "stack_done",
            "sg_ready", "tok_ready", "sc_ready", "ex_ready", "batch_done",
            "h_full", "relu_done", "y_full", "y_used", "o_ready",
        ):
            sem(name)

        def tally(name, start=0, step=1):
            return Tally(name, sems[name], start, step)

        def signal(name, step=1):
            return Signal(sems[name], step)

        DMAS = 16

        def apart(engine):
            engine.sem_inc(sems["apart"], 1)

        block = ctx.enter_context(nc.Block())

        @block.sync
        def _(sp):
            loaded, xb_loaded = signal("loaded", step=DMAS), signal("xb_loaded", step=DMAS)
            w0_loaded = tally("w0_loaded", step=DMAS)
            rows0, rows1 = signal("rows0_loaded", step=DMAS), signal("rows1_loaded", step=DMAS)
            we_loaded = [tally("we0_loaded", step=DMAS), tally("we1_loaded", step=DMAS)]
            stored = [tally("stored0", DMAS, DMAS), tally("stored1", DMAS, DMAS)]
            hi_done, rows_ready = tally("hi_done"), tally("rows_ready")
            y_full, o_ready = tally("y_full"), tally("o_ready")
            every = [w0_loaded, *we_loaded, *stored, hi_done,
                     rows_ready, y_full, o_ready]

            def max_rows0(u):
                sp.wait_ge(rows_ready.sem, rows_ready.next())
                sp.dma_start(ops0[64:65, u, QB, 0, :].bitcast(F32), mrows[0:TILES, :].bitcast(F32)).then_inc(rows0.sem, rows0.up())
                sp.dma_start(ops0[0:1, u, QB, 1, :].bitcast(F32),
                             mrows[TILES:2 * TILES, :].bitcast(F32)).then_inc(rows0.sem, rows0.up())

            def load_w0(p):
                sp.dma_start(w0[:].rearrange("p k c -> p (k c)"),
                             wl0[bass.ds(p, 1)].rearrange("o p c -> (o p) c")).then_inc(w0_loaded.sem, w0_loaded.up())

            def max_rows1(u):
                sp.wait_ge(rows_ready.sem, rows_ready.next())
                for g in range(GH):
                    r = 32 * g + 24
                    sp.dma_start(ops1[r:r + 1, u, GH, :].bitcast(F32),
                                 mrows[TILES * g:TILES * (g + 1), :].bitcast(F32)).then_inc(rows1.sem, rows1.up())

            sp.sem_inc(sems["stored0"], DMAS)
            sp.sem_inc(sems["stored1"], DMAS)
            sp.dma_start(cst[:], pack).then_inc(loaded.sem, loaded.up())
            sp.dma_start(tabs[:, 0:2 * T], rope).then_inc(loaded.sem, loaded.up())
            sp.dma_start(wfi, wffn).then_inc(loaded.sem, loaded.up())
            with repeat(sp, "batch", B, every) as b:
                sp.wait_ge(sems["batch_done"], b + 1)
                sp.dma_start(xb[:].rearrange("p n d -> p (n d)"),
                             x_in[:, bass.ds(b * TILES * D, TILES * D)]).then_inc(xb_loaded.sem, xb_loaded.up())
                load_w0(0)
                sp.wait_ge(hi_done.sem, hi_done.next(8))
                load_w0(1)
                max_rows0(0)
                with repeat(sp, "pairs", PAIRS // 2 - 1, every) as j:
                    for u in (1, 0):
                        sp.wait_ge(hi_done.sem, hi_done.next(8))
                        load_w0(2 * j + 3 - u)
                        max_rows0(u)
                max_rows0(1)
                hi_done.count(8)
                for n in range(GROUPS):
                    max_rows1(n % 2)
            sp.wait_ge(sems["batch_done"], B + 1)
            for e in range(2):
                sp.dma_start(we[:, e, :], wmoe[e]).then_inc(we_loaded[e].sem, we_loaded[e].up())
            with repeat(sp, "experts", EXPERTS // 2 - 1, every) as j:
                for u in range(2):
                    sp.wait_ge(y_full.sem, y_full.next(TILES))
                    sp.dma_start(we[:, u, :], wmoe[bass.ds(2 * j + 2 + u, 1)]
                                 .rearrange("o p c -> (o p) c")).then_inc(we_loaded[u].sem, we_loaded[u].up())
            with repeat(sp, "last", TILES // 2, every) as j:
                for u in range(2):
                    sp.wait_ge(o_ready.sem, o_ready.next())
                    sp.dma_start(out[bass.ds(2 * j + u, 1)].rearrange("o p c -> (o p) c"),
                                 ocur[:, u].rearrange("p s d -> p (s d)")).then_inc(stored[u].sem, stored[u].up())
            for u in range(2):
                sp.wait_ge(stored[u].sem, stored[u].seen())

        @block.tensor
        def _(pe):
            ms_free, ms_dve, ms_act = tally("ms_free"), signal("ms_dve"), signal("ms_act")
            xn_ready = tally("xn_ready")
            w0_loaded = tally("w0_loaded", step=DMAS)
            rows0, rows1 = tally("rows0_loaded", step=DMAS), tally("rows1_loaded", step=DMAS)
            st_full, st_free, p_ready, p_used = (
                signal("st_full"), tally("p_ready"), tally("p_ready", start=2), signal("p_used"))
            av_full, av_free, av1_free = signal("av_full"), tally("av_free"), tally("av1_free")
            hi_done, qlo_done, klo_done = tally("hi_done"), tally("qlo_done"), tally("klo_done")
            rope_done = tally("rope_done")
            rows_ready, stack_done, hi1_done = tally("rows_ready"), tally("stack_done"), tally("hi1_done")
            outT_ready, tok_ready, pool_prep = tally("outT_ready"), tally("tok_ready"), tally("pool_prep")
            h_full, relu_done, relu_free = tally("h_full"), tally("relu_done", start=4), tally("relu_done")
            y_full, y_free = signal("y_full"), tally("y_used")
            we_loaded = [tally("we0_loaded", step=DMAS), tally("we1_loaded", step=DMAS)]
            every = [ms_free, xn_ready, w0_loaded, rows0, rows1, st_free,
                     p_ready, av_free, av1_free, hi_done, qlo_done, klo_done, rows_ready, stack_done,
                     rope_done, hi1_done, outT_ready, tok_ready, pool_prep, h_full, relu_done, relu_free, y_free,
                     *we_loaded]
            pe.sem_inc(sems["p_used"], 1)

            def transposed(source, n):
                pe.wait_ge(ms_free.sem, ms_free.next())
                for i in range(n):
                    mm = nc.tensor.transpose(ms3[:, i, :], source(i), at["ident"])
                mm.then_inc(ms_act.sem, ms_act.up())

            def project0(k, c):
                if k == 0 and c == 0:
                    pe.wait_ge(w0_loaded.sem, w0_loaded.next())
                    pe.wait_ge(ms_free.sem, ms_free.seen(1))
                elif c == 1:
                    pe.wait_ge(rope_done.sem, rope_done.next())
                for r in range(2):
                    mm = nc.tensor.matmul(ms[:, r * CH:(r + 1) * CH], w0[:, k + r, :],
                                          xT[:, c * CH:(c + 1) * CH], start=True, stop=True)
                mm.then_inc(ms_dve.sem, ms_dve.up())

            def values0():
                pe.wait_ge(rope_done.sem, rope_done.next())
                pe.wait_ge(ms_free.sem, ms_free.next())
                for i in range(TILES):
                    mm = nc.tensor.matmul(ms3[:, i, :], xT[:, i * P:(i + 1) * P], w0[:, 4, :],
                                          start=True, stop=True)
                mm.then_inc(ms_act.sem, ms_act.up())

            def scores_qk0(u, h, i, first=False):
                for c in range(i // 4 + 1):
                    pe.wait_ge(ms_free.sem, ms_free.next() - (0 if first and c == 0 else 1))
                    half = c * CH if i >= 4 else h * CH
                    diagonal = c == i // 4
                    n = (i % 4 + 1) * P if diagonal else CH
                    mm = nc.tensor.matmul(ms[:, half:half + n], ops0[:, u, QA, h, i * P:(i + 1) * P],
                                          ops0[:, u, KA, h, c * CH:c * CH + n], start=True, stop=True)
                    if diagonal:
                        mm = nc.tensor.matmul(ms[:, half + n - P:half + n], ident_r[:], mask_qk[:], start=False,
                                              stop=True, skip_group_check=True)
                    mm.then_inc(ms_dve.sem, ms_dve.up())

            def maxima(n):
                pe.wait_ge(ms_free.sem, ms_free.seen(1))
                mm = nc.tensor.transpose(ms[0:n, 0:P], mx[:, 0, 0:n], at["ident"])
                mm.then_inc(ms_act.sem, ms_act.up())
                pe.wait_ge(rows_ready.sem, rows_ready.next())

            def chunks(kt):
                return [(max(c * CH, kt * P), (c + 1) * CH) for c in range(kt // 4, 2)]

            def scores_st0(u, h, kt):
                pe.wait_ge(st_free.sem, st_free.next())
                for a, z in chunks(kt):
                    diagonal = a == kt * P
                    nc.tensor.matmul(st[:, kt % 2, a:z], ops0[:, u, KA, h, kt * P:(kt + 1) * P],
                                     ops0[:, u, QA, h, a:z], start=True, stop=False)
                    mm = nc.tensor.matmul(st[:, kt % 2, a:z], ops0[:, u, KB, h, kt * P:(kt + 1) * P],
                                          ops0[:, u, QB, h, a:z], start=False, stop=True)
                    if diagonal:
                        mm = nc.tensor.matmul(st[:, kt % 2, a:a + P], ident_r[:], mask_st[:], start=False,
                                              stop=True, skip_group_check=True)
                mm.then_inc(st_full.sem, st_full.up())

            def weigh0(u, h, kt):
                pe.wait_ge(p_ready.sem, p_ready.next())
                for a, z in chunks(kt):
                    if kt == 0:
                        pe.wait_ge(av_free.sem, av_free.next())
                    last = kt == z // P - 1
                    mm = nc.tensor.matmul(av[:, a:z], v0[:, u, kt, h, :], p0[:, kt % 2, a:z],
                                          start=(kt == 0), stop=last)
                    if last:
                        mm.then_inc(av_full.sem, av_full.up())
                if kt < TILES - 1:
                    mm.then_inc(p_used.sem, p_used.up())

            def pair(u, following, further):
                pe.wait_ge(klo_done.sem, klo_done.next(2))
                pe.wait_ge(rows0.sem, rows0.next(2))
                scores_st0(u, 0, 0)
                for s in range(2 * TILES):
                    if s + 1 < 2 * TILES:
                        scores_st0(u, *divmod(s + 1, TILES))
                    weigh0(u, *divmod(s, TILES))
                    if following:
                        if s == 2:
                            pe.wait_ge(rope_done.sem, rope_done.next())
                            project0(2, 0)
                        if s == 4:
                            project0(2, 1)
                        if s == 5:
                            values0()
                        if s == TILES:
                            pe.wait_ge(hi_done.sem, hi_done.next(8))
                            pe.wait_ge(qlo_done.sem, qlo_done.next(2))
                        if s >= TILES:
                            for h in range(2):
                                scores_qk0(1 - u, h, 2 * TILES - 1 - s, first=(s == TILES and h == 0))
                if following:
                    maxima(2 * TILES)
                if further:
                    project0(0, 0)
                    project0(0, 1)

            def project1(n, k):
                if k == 0:
                    pe.wait_ge(ms_free.sem, ms_free.seen(1))
                else:
                    pe.wait_ge(hi1_done.sem, hi1_done.next())
                w = at["wqk1"][:, (2 * n + k) * P:(2 * n + k + 1) * P]
                for c in range(2):
                    mm = nc.tensor.matmul(ms[:, c * CH:(c + 1) * CH], w, xT[:, c * CH:(c + 1) * CH],
                                          start=True, stop=True)
                mm.then_inc(ms_act.sem, ms_act.up())

            def scores_qk1(u, g, i, first=False):
                for c in range(2):
                    pe.wait_ge(ms_free.sem, ms_free.next() - (0 if first and c == 0 else 1))
                    nc.tensor.matmul(ms[:, c * CH:(c + 1) * CH], ops1[:, u, GH, i * P:(i + 1) * P],
                                     ops1[:, u, g, c * CH:(c + 1) * CH], start=True,
                                     stop=True).then_inc(ms_dve.sem, ms_dve.up())

            def scores_st1(u, kt, g):
                pe.wait_ge(st_free.sem, st_free.next())
                for c in range(2):
                    mm = nc.tensor.matmul(st[:, g % 2, c * CH:(c + 1) * CH],
                                          ops1[:, u, g, kt * P:(kt + 1) * P],
                                          ops1[:, u, GH, c * CH:(c + 1) * CH], start=True, stop=True)
                mm.then_inc(st_full.sem, st_full.up())

            def weigh1(head, kt):
                pe.wait_ge(p_ready.sem, p_ready.next(GH))
                if kt == 0 and head > 0:
                    pe.wait_ge(av1_free.sem, av1_free.next())
                for c in range(2):
                    for g in range(GH):
                        mm = nc.tensor.matmul(av[32 * g:32 * g + 32, c * CH:(c + 1) * CH],
                                              v1[:, kt, head + g, :], p1[:, kt % 2, g, c * CH:(c + 1) * CH],
                                              start=(kt == 0), stop=(kt == TILES - 1), skip_group_check=True)
                if kt == TILES - 1:
                    mm.then_inc(av_full.sem, av_full.up())
                else:
                    mm.then_inc(p_used.sem, p_used.up())

            def finish1():
                pe.wait_ge(ms_free.sem, ms_free.next())
                for i in range(TILES):
                    mm = nc.tensor.transpose(ms3[:, i, :], p0[:, 0, i * P:(i + 1) * P], at["ident"])
                mm.then_inc(ms_dve.sem, ms_dve.up())

            def group(n):
                u, following = n % 2, n < GROUPS - 1
                if following:
                    project1(n + 1, 0)
                pe.wait_ge(rows1.sem, rows1.next(GH))
                scores_st1(u, 0, 0)
                for s in range(GH * TILES):
                    kt, g = divmod(s + 1, GH)
                    if kt < TILES:
                        scores_st1(u, kt, g)
                    if s == 0 and following:
                        project1(n + 1, 1)
                    if s % GH == 1 and s > GH:
                        weigh1(n * GH, s // GH - 1)
                    if s == GH + 1 and following:
                        pe.wait_ge(hi1_done.sem, hi1_done.next())
                    if s == GH + 2 and n > 0:
                        finish1()
                    if following and s > GH + 2:
                        first = 2 * (s - GH - 3) if s < 14 else s
                        for m in range(first, first + (2 if s < 14 else 1)):
                            if m == 0:
                                pe.wait_ge(stack_done.sem, stack_done.next())
                            if m % TILES == 0:
                                pe.wait_ge(stack_done.sem, stack_done.next())
                            scores_qk1(1 - u, *divmod(m, TILES), first=(m == 0))
                weigh1(n * GH, TILES - 1)
                if following:
                    maxima(GH * TILES)

            pe.wait_ge(sems["loaded"], 3 * DMAS)
            pe.wait_ge(sems["prep_done"], 5)
            with repeat(pe, "batch", B, every):
                pe.wait_ge(xn_ready.sem, xn_ready.next())
                transposed(lambda i: xn[:, i, :], TILES)
                project0(0, 0)
                project0(0, 1)
                pe.wait_ge(rope_done.sem, rope_done.next())
                project0(2, 0)
                project0(2, 1)
                values0()
                pe.wait_ge(hi_done.sem, hi_done.next(8))
                pe.wait_ge(qlo_done.sem, qlo_done.next(2))
                for i in reversed(range(TILES)):
                    for h in range(2):
                        scores_qk0(0, h, i, first=(i == TILES - 1 and h == 0))
                maxima(2 * TILES)
                project0(0, 0)
                project0(0, 1)
                pe.wait_ge(pool_prep.sem, pool_prep.next())
                apart(pe)
                with repeat(pe, "pairs", PAIRS // 2 - 1, every):
                    for u in range(2):
                        pair(u, True, True)
                pair(0, True, False)
                pair(1, False, False)
                pe.wait_ge(outT_ready.sem, outT_ready.next())
                pe.wait_ge(ms_free.sem, ms_free.seen(1))
                for i in range(TILES):
                    for p in range(PAIRS):
                        mm = nc.tensor.matmul(ms3[:, i, :], outT[:, p, i * P:(i + 1) * P],
                                              at["wo0"][:, p * D:(p + 1) * D],
                                              start=(p == 0), stop=(p == PAIRS - 1))
                mm.then_inc(ms_dve.sem, ms_dve.up())
                pe.wait_ge(xn_ready.sem, xn_ready.next())
                transposed(lambda i: xn[:, i, :], TILES)
                for f in range(FT):
                    for c in range(2):
                        pe.wait_ge(ms_free.sem, ms_free.next())
                        for r in range(2):
                            mm = nc.tensor.matmul(ms[:, r * CH:(r + 1) * CH], wf[:, r * FT + f, :],
                                                  xT[:, c * CH:(c + 1) * CH], start=True, stop=True)
                        mm.then_inc(ms_act.sem, ms_act.up())
                pe.wait_ge(ms_free.sem, ms_free.seen(1))
                for i in range(TILES):
                    for f in range(FT):
                        mm = nc.tensor.matmul(ms3[:, i, :], hT[:, f, i * P:(i + 1) * P], wf[:, 2 * FT + f, :],
                                              start=(f == 0), stop=(f == FT - 1))
                mm.then_inc(ms_dve.sem, ms_dve.up())
                pool_prep.count()
                pe.wait_ge(xn_ready.sem, xn_ready.next())
                transposed(lambda i: xn[:, i, :], TILES)
                pe.wait_ge(ms_free.sem, ms_free.next())
                for i in range(TILES):
                    mm = nc.tensor.matmul(ms3[:, i, :], xT[:, i * P:(i + 1) * P], at["wv1"],
                                          start=True, stop=True)
                mm.then_inc(ms_dve.sem, ms_dve.up())
                project1(0, 0)
                project1(0, 1)
                pe.wait_ge(hi1_done.sem, hi1_done.next())
                pe.wait_ge(stack_done.sem, stack_done.next())
                for g in range(GH):
                    pe.wait_ge(stack_done.sem, stack_done.next())
                    for i in range(TILES):
                        scores_qk1(0, g, i, first=(g == 0 and i == 0))
                maxima(GH * TILES)
                for n in range(GROUPS):
                    group(n)
                pe.wait_ge(av1_free.sem, av1_free.next())
                finish1()
                pe.wait_ge(ms_free.sem, ms_free.seen(1))
                transposed(lambda i: y[:, i, :], TILES)
                pe.wait_ge(ms_free.sem, ms_free.seen(1))
                for i in range(TILES):
                    mm = nc.tensor.matmul(ms3[:, i, :], xT[:, i * P:(i + 1) * P], at["wo1"],
                                          start=True, stop=True)
                mm.then_inc(ms_dve.sem, ms_dve.up())

            with repeat(pe, "tokens", TILES, every):
                pe.wait_ge(xn_ready.sem, xn_ready.next())
                transposed(lambda i: xn[:, i, :], B)
                for half in range(2):
                    if half == 0:
                        pe.wait_ge(ms_free.sem, ms_free.next())
                    else:
                        pe.wait_ge(ms_free.sem, ms_free.seen(1))
                    for r in range(2):
                        s = 2 * half + r
                        mm = nc.tensor.matmul(ms[:, r * CH:r * CH + 3 * D], sT[:, s * P:(s + 1) * P],
                                              at["win"], start=True, stop=True)
                    mm.then_inc(ms_dve.sem, ms_dve.up())
                pe.wait_ge(tok_ready.sem, tok_ready.next())
                transposed(lambda i: y[:, i, :], B)
                pe.wait_ge(ms_free.sem, ms_free.seen(1))
                for s in range(B):
                    mm = nc.tensor.matmul(ms3[:, s, :], cT[:, s * P:(s + 1) * P], at["wout"],
                                          start=True, stop=True)
                mm.then_inc(ms_dve.sem, ms_dve.up())
                pe.wait_ge(xn_ready.sem, xn_ready.next())
                transposed(lambda i: y[:, i, :], B)
                pe.wait_ge(ms_free.sem, ms_free.seen(1))
                for s in range(B):
                    mm = nc.tensor.matmul(ms[:, s * EXPERTS:(s + 1) * EXPERTS], xT[:, s * P:(s + 1) * P],
                                          at["wgate"], start=True, stop=True)
                mm.then_inc(ms_dve.sem, ms_dve.up())
                pe.wait_ge(tok_ready.sem, tok_ready.next())
                pe.wait_ge(ms_free.sem, ms_free.next())
                for s in range(B):
                    mm = nc.tensor.transpose(ms[0:EXPERTS, s * P:(s + 1) * P], gt[7][:, s, :], at["ident"])
                mm.then_inc(ms_act.sem, ms_act.up())
                pe.wait_ge(ms_free.sem, ms_free.seen(1))
                for s in range(B):
                    mm = nc.tensor.matmul(ms3[:, s, :], cbT[0:EXPERTS, s * P:(s + 1) * P],
                                          at["b2"][0:EXPERTS, :], start=True, stop=True)
                mm.then_inc(ms_dve.sem, ms_dve.up())

            def hidden(e, chunk):
                for f in range(4):
                    pe.wait_ge(relu_free.sem, relu_free.next())
                    nc.tensor.matmul(st[:, f // 2, f % 2 * CH:(f % 2 + 1) * CH],
                                     we[:, e, f * P:(f + 1) * P], x1T[:, bass.ds(chunk * CH, CH)],
                                     start=True, stop=True).then_inc(h_full.sem, h_full.up())

            def expert_out(e, u, last):
                pe.wait_ge(relu_done.sem, relu_done.next(4))
                pe.wait_ge(y_free.sem, y_free.next())
                for s in range(B):
                    for f in range(4):
                        mm = nc.tensor.matmul(av[:, u * CH + s * D:u * CH + (s + 1) * D],
                                              relu[:, u, f, s * P:(s + 1) * P],
                                              we[:, e, HID + f * D:HID + (f + 1) * D],
                                              start=(f == 0), stop=(f == 3))
                mm.then_inc(y_full.sem, y_full.up())

            pe.wait_ge(ms_free.sem, ms_free.seen(1))
            apart(pe)
            with repeat(pe, "experts", EXPERTS // 2, every):
                for e in range(2):
                    pe.wait_ge(we_loaded[e].sem, we_loaded[e].next())
                    apart(pe)
                    with repeat(pe, "chunks", TILES // 2, every) as j:
                        hidden(e, 2 * j)
                        hidden(e, 2 * j + 1)
                        expert_out(e, 0, False)
                        expert_out(e, 1, False)

        @block.scalar
        def _(act):
            own = tally("act_own")
            ms_act, st_full, p_used = tally("ms_act"), tally("st_full"), tally("p_used")
            p_ready, av_full = signal("p_ready"), tally("av_full")
            rope_done, hi_done, rows_ready = tally("rope_done"), tally("hi_done"), tally("rows_ready")
            hi1_done, sg_ready, ms_free, av_free, av1_free = (
                signal("hi1_done"), signal("sg_ready"), signal("ms_free"), signal("av_free"), signal("av1_free"))
            sc_ready, ex_ready, h_full, relu_done = (
                tally("sc_ready"), signal("ex_ready"), tally("h_full"), signal("relu_done"))
            every = [own, ms_act, st_full, p_used, av_full, rope_done, hi_done, rows_ready,
                     sc_ready, h_full]
            act.sem_inc(sems["p_ready"], 2)
            act.sem_inc(sems["relu_done"], 4)

            act.sem_inc(sems["av_free"], 2)

            def copy(dst, src):
                return nc.scalar.activation(dst, src, ACT.Copy)

            def drain(dst, src):
                act.wait_ge(ms_act.sem, ms_act.next())
                copy(dst, src).then_inc(ms_free.sem, ms_free.up())

            def hi0(u, k, which):
                src = (qs, ks)[k]
                low, high = slice(0, 64), slice(64, P)
                moves = ([(low, low, QA, 0), (high, high, QA, 1), (low, low, QB, 0), (high, high, QB, 1)],
                         [(low, low, KA, 0), (high, low, KA, 0), (high, high, KA, 1), (low, high, KA, 1)])[k]
                for m in which:
                    to, frm, part, h = moves[m]
                    if m == 0:
                        act.wait_ge(rope_done.sem, rope_done.next(2))
                    copy(ops0[to, u, part, h, :], src[frm]).then_inc(hi_done.sem, hi_done.up())

            def values0(u):
                act.wait_ge(ms_act.sem, ms_act.next())
                copy(v0[:, u, :, 0, 0:C0], ms3[:, :, 0:C0])
                copy(v0[:, u, :, 1, C0:P], ms3[:, :, C0:P]).then_inc(ms_free.sem, ms_free.up())

            def exponentials0(kt):
                act.wait_ge(st_full.sem, st_full.next())
                if kt != 1:
                    act.wait_ge(p_used.sem, p_used.next())
                nc.scalar.activation(p0[:, kt % 2, kt * P:T], st[:, kt % 2, kt * P:T], ACT.Exp,
                                     scale=SCALE0).then_inc(p_ready.sem, p_ready.up())

            def drain_av(u, h, p, c):
                values, ones = (slice(0, 64), slice(64, P)) if h == 0 else (slice(64, P), slice(0, 64))
                cols = slice(c * CH, (c + 1) * CH)
                act.wait_ge(av_full.sem, av_full.next())
                copy(sums[values, u, cols], av[ones, cols])
                copy(outT[values, bass.ds(p, 1), cols].rearrange("r o t -> r (o t)"),
                     av[values, cols]).then_inc(av_free.sem, av_free.up())

            def minus_maxima(n):
                act.wait_ge(ms_act.sem, ms_act.next())
                nc.scalar.mul(mrows[0:n, :], ms[0:n, 0:P], -1.0).then_inc(rows_ready.sem, rows_ready.up())

            def pair(u, p, following):
                for s in range(2 * TILES):
                    h, kt = divmod(s, TILES)
                    exponentials0(kt)
                    if kt == TILES // 2:
                        drain_av(u, h, p, 0)
                    if s == TILES:
                        drain_av(u, 0, p, 1)
                    if following:
                        if s < 4:
                            hi0(1 - u, 0, [s])
                        if s == 6:
                            values0(1 - u)
                            hi0(1 - u, 1, [0, 1])
                        if s == 7:
                            hi0(1 - u, 1, [2, 3])
                drain_av(u, 1, p, 1)
                if following:
                    minus_maxima(2 * TILES)

            def biased(n, k):
                act.wait_ge(ms_act.sem, ms_act.next())
                high_scale, whole_scale = at[("qc", "kc")[k]], at[("qb", "kb")[k]]
                nc.scalar.activation((xq, xk)[k], ms[:], ACT.Identity, scale=whole_scale,
                                     bias=bias_whole[:, 2 * n + k:2 * n + k + 1])
                nc.scalar.activation((hq, hk)[k].bitcast(F32R), ms[:], ACT.Identity, scale=high_scale,
                                     bias=bias_high[:, 2 * n + k:2 * n + k + 1]).then_inc(hi1_done.sem, hi1_done.up())

            def group(n):
                following = n < GROUPS - 1
                if following:
                    biased(n + 1, 0)
                for s in range(GH * TILES):
                    kt, g = divmod(s, GH)
                    act.wait_ge(st_full.sem, st_full.next())
                    if g == 0 and kt != 1:
                        act.wait_ge(p_used.sem, p_used.next())
                    nc.scalar.activation(p1[:, kt % 2, g, :], st[:, g % 2, :], ACT.Exp,
                                         scale=SCALE1).then_inc(p_ready.sem, p_ready.up())
                    if following and s == 1:
                        biased(n + 1, 1)
                    if n > 0 and s == GH - 1:
                        values_out()
                if following:
                    minus_maxima(GH * TILES)

            def values_out():
                act.wait_ge(av_full.sem, av_full.next())
                copy(p0[:, 0, :], av[:]).then_inc(av1_free.sem, av1_free.up())

            act.wait_ge(sems["loaded"], 3 * DMAS)
            act.wait_ge(sems["prep_done"], 5)
            with repeat(act, "batch", B, every):
                drain(xT[:], ms[:])
                hi0(0, 0, range(4))
                values0(0)
                hi0(0, 1, range(4))
                minus_maxima(2 * TILES)
                with repeat(act, "pairs", PAIRS // 2 - 1, every) as j:
                    for u in range(2):
                        pair(u, 2 * j + u, True)
                pair(0, PAIRS - 2, True)
                pair(1, PAIRS - 1, False)
                drain(xT[:], ms[:])
                for _ in range(2 * FT):
                    act.wait_ge(ms_act.sem, ms_act.next())
                    nc.scalar.activation(sg, ms[:, 0:CH], ACT.Silu).then_inc(sg_ready.sem, sg_ready.up())
                drain(xT[:], ms[:])
                for k in range(2):
                    biased(0, k)
                minus_maxima(GH * TILES)
                for n in range(GROUPS):
                    group(n)
                values_out()
                drain(xT[:], ms[:])

            with repeat(act, "tokens", TILES, every) as i:
                drain(sT, ms[:, 0:CH])
                act.wait_ge(sc_ready.sem, sc_ready.next())
                nc.scalar.activation(ex, sc, ACT.Exp, scale=SCALE2).then_inc(ex_ready.sem, ex_ready.up())
                drain(cT, ms[:, 0:CH])
                act.wait_ge(ms_act.sem, ms_act.next())
                copy(x1T[:, bass.ds(i * CH, CH)], ms[:, 0:CH])
                copy(xT[:, 0:CH], ms[:, 0:CH]).then_inc(ms_free.sem, ms_free.up())
                act.wait_ge(sc_ready.sem, sc_ready.next())
                nc.scalar.activation(gt[1], gt[0], ACT.Exp).then_inc(ex_ready.sem, ex_ready.up())
                drain(cbT[0:EXPERTS, :], ms[0:EXPERTS, 0:CH])

            with repeat(act, "experts", EXPERTS // 2, every):
                for e in range(2):
                    with repeat(act, "chunks", TILES // 2, every):
                        for u in range(2):
                            for f in range(4):
                                act.wait_ge(h_full.sem, h_full.next())
                                b1 = we[:, e, 2 * HID + f:2 * HID + f + 1]
                                nc.scalar.activation(relu[:, u, f, :],
                                                     st[:, f // 2, f % 2 * CH:(f % 2 + 1) * CH],
                                                     ACT.Relu, bias=b1).then_inc(relu_done.sem, relu_done.up())

        @block.gpsimd
        def _(pool):
            own, var_ready, rstd_ready = tally("pool_own"), tally("var_ready"), signal("rstd_ready")
            prep, outT_ready, hi_done, klo_done = (
                tally("pool_prep"), tally("outT_ready"), tally("hi_done"), tally("klo_done"))
            hi1_done, stack_done = tally("hi1_done"), tally("stack_done")
            every = [own, var_ready, prep, outT_ready, hi_done, klo_done, hi1_done, stack_done]
            low, high = slice(0, 64), slice(64, P)

            def inverse_roots():
                pool.wait_ge(var_ready.sem, var_ready.next())
                nc.gpsimd.tensor_tensor(rstd[:], var[:], neghalf[:].broadcast_to([P, TILES]), ALU.pow).then_inc(rstd_ready.sem, rstd_ready.up())

            def klo(u):
                pool.wait_ge(hi_done.sem, hi_done.next(8))
                for h, rows in ((0, low), (1, high)):
                    nc.gpsimd.tensor_tensor(
                        ops0[rows, u, KB, h, :], ks[rows],
                        ops0[rows, u, KA, h, :].bitcast(F32), ALU.subtract).then_inc(klo_done.sem, klo_done.up())
                pool.wait_ge(klo_done.sem, klo_done.seen())
                apart(pool)

            def stack(u, k):
                pool.wait_ge(hi1_done.sem, hi1_done.next())
                x, h = (xq, xk)[k], (hq, hk)[k]
                if k == 0:
                    nc.gpsimd.tensor_tensor(ops1[:, u, GH, :], h, x, ALU.add).then_inc(stack_done.sem,
                                                                                       stack_done.up())
                else:
                    for g in range(GH):
                        r = slice(32 * g, 32 * g + 32)
                        nc.gpsimd.tensor_tensor(ops1[r, u, g, :], h[r], x[r], ALU.add).then_inc(
                            stack_done.sem, stack_done.up())
                pool.wait_ge(stack_done.sem, stack_done.seen())
                apart(pool)

            nc.gpsimd.memset(neghalf[:], -0.5).then_inc(own.sem, own.up())
            pool.wait_ge(own.sem, own.seen())
            pool.wait_ge(sems["loaded"], 3 * DMAS)
            with repeat(pool, "batch", B, every) as b:
                pool.wait_ge(sems["batch_done"], b + 1)
                apart(pool)
                for u in range(2):
                    nc.gpsimd.memset(v0[:, u, :, 0, C0:P], 1.0).then_inc(own.sem, own.up())
                    nc.gpsimd.memset(v0[:, u, :, 1, 0:C0], 1.0).then_inc(own.sem, own.up())
                pool.wait_ge(own.sem, own.seen())
                apart(pool)
                for u in range(2):
                    for k in (QB, KB):
                        nc.gpsimd.memset(ops0[high, u, k, 0, :].bitcast(F32), 0.0).then_inc(own.sem, own.up())
                        nc.gpsimd.memset(ops0[low, u, k, 1, :].bitcast(F32), 0.0).then_inc(own.sem, own.up())
                pool.wait_ge(own.sem, own.seen())
                apart(pool)
                for u in range(2):
                    nc.gpsimd.memset(ops0[64:65, u, KB, 0, :].bitcast(F32), 1.0).then_inc(own.sem, own.up())
                    nc.gpsimd.memset(ops0[0:1, u, KB, 1, :].bitcast(F32), 1.0).then_inc((own, prep)[u].sem, (own, prep)[u].up())
                pool.wait_ge(prep.sem, prep.seen())
                apart(pool)
                inverse_roots()
                klo(0)
                with repeat(pool, "pairs", PAIRS // 2 - 1, every):
                    klo(1)
                    klo(0)
                klo(1)
                inverse_roots()
                inverse_roots()
                pool.wait_ge(outT_ready.sem, outT_ready.next())
                apart(pool)
                nc.gpsimd.memset(parts[:, 0:10].bitcast(F32), 0.0).then_inc(own.sem, own.up())
                nc.gpsimd.memset(vals[:], 0.0).then_inc(own.sem, own.up())
                pool.wait_ge(own.sem, own.seen())
                apart(pool)
                nc.gpsimd.memset(v1[:, :, :, C1:C1 + 1], 1.0).then_inc(prep.sem, prep.up())
                inverse_roots()
                inverse_roots()
                for n in range(GROUPS):
                    stack(n % 2, 0)
                    stack(n % 2, 1)
                inverse_roots()

            with repeat(pool, "tokens", TILES, every):
                inverse_roots()
                inverse_roots()
            with repeat(pool, "last", TILES // 2, every):
                for _ in range(4):
                    inverse_roots()

        @block.vector
        def _(dve):
            own, ms_dve, ms_free = tally("dve_own"), tally("ms_dve"), signal("ms_free")
            xb_loaded, var_ready, rstd_ready, xn_ready = (
                tally("xb_loaded", step=DMAS), tally("var_ready"), tally("rstd_ready"), tally("xn_ready"))
            rope_done, hi_done, qlo_done = signal("rope_done"), tally("hi_done"), signal("qlo_done")
            av_free, outT_ready = tally("av_free", start=2), tally("outT_ready")
            sg_ready, pool_prep, tok_ready = tally("sg_ready"), tally("pool_prep"), tally("tok_ready")
            sc_ready, ex_ready, batch_done = tally("sc_ready"), tally("ex_ready"), tally("batch_done")
            y_full, y_used, o_ready = tally("y_full"), tally("y_used"), tally("o_ready")
            stored = [tally("stored0", step=DMAS), tally("stored1", step=DMAS)]
            every = [own, ms_dve, xb_loaded, var_ready, rstd_ready, xn_ready, hi_done,
                     av_free, outT_ready, sg_ready, pool_prep, tok_ready, sc_ready,
                     ex_ready, batch_done, y_full, y_used, o_ready, *stored]
            low, high = slice(0, 64), slice(64, P)
            dve.sem_inc(sems["ms_free"], 1)
            dve.sem_inc(sems["batch_done"], 1)
            dve.sem_inc(sems["y_used"], 2)

            def tt(dst, a, b, op):
                return nc.vector.tensor_tensor(dst, a, b, op)

            def normalise(n, source, dst, done=None):
                for i in range(n):
                    last = nc.vector.bn_stats(stats[:, i, :], source(i))
                last.then_inc(own.sem, own.up())
                dve.wait_ge(own.sem, own.seen())
                apart(dve)
                for i in range(n):
                    last = nc.vector.bn_aggr(mv[:, i, :], stats[:, i, :])
                last.then_inc(own.sem, own.up())
                dve.wait_ge(own.sem, own.seen())
                nc.vector.tensor_scalar(var[:, 0:n], mv[:, 0:n, 1], EPS, None, ALU.add).then_inc(var_ready.sem, var_ready.up())
                dve.wait_ge(rstd_ready.sem, rstd_ready.next())
                for i in range(n):
                    last = nc.vector.tensor_scalar(dst(i), source(i), mv[:, i, 0:1], rstd[:, i:i + 1],
                                                   ALU.subtract, ALU.mult)
                last.then_inc((done or own).sem, (done or own).up())
                if done is None:
                    dve.wait_ge(own.sem, own.seen())

            def over(row, n):
                return row.unsqueeze(1).broadcast_to([P, n, D])

            def rope(k, c):
                dve.wait_ge(ms_dve.sem, ms_dve.next())
                cols = slice(c * CH, (c + 1) * CH)
                tt(t1, ms[:, 0:CH], cosT[:, cols], ALU.mult)
                tt(t2, ms[:, CH:T], sinT[:, cols], ALU.mult).then_inc(own.sem, own.up())
                dve.wait_ge(own.sem, own.seen())
                tt((qs, ks)[k][:, cols], t1, t2, ALU.add).then_inc(rope_done.sem, rope_done.up())

            def qlo(u):
                dve.wait_ge(hi_done.sem, hi_done.next(4))
                hi_done.count(4)
                for h, frm, to in ((0, low, high), (1, high, low)):
                    tt(ops0[to, u, QA, h, :], qs[frm], ops0[frm, u, QA, h, :].bitcast(F32),
                       ALU.subtract).then_inc(qlo_done.sem, qlo_done.up())

            def row_max(c, column, half, n, last=False):
                dve.wait_ge(ms_dve.sem, ms_dve.next())
                done = nc.vector.tensor_reduce(mx[:, c, column:column + 1], ms[:, half * CH:half * CH + n], AX.X,
                                               ALU.max)
                if last:
                    done.then_inc(own.sem, own.up())
                    dve.wait_ge(own.sem, own.seen())
                else:
                    done.then_inc(ms_free.sem, ms_free.up())

            def maxima0():
                for i in reversed(range(TILES)):
                    for h in range(2):
                        column = h * TILES + i
                        if i >= 4:
                            row_max(0, column, 0, CH)
                            row_max(1, column, 1, (i - 3) * P)
                        else:
                            row_max(0, column, h, (i + 1) * P, last=(i == 0 and h == 1))
                both = [mx[:, c, 0:2 * TILES].rearrange("p (h i) -> p h i", i=TILES)[:, :, 4:TILES] for c in range(2)]
                tt(both[0], both[0], both[1], ALU.max).then_inc(ms_free.sem, ms_free.up())

            def divide(u, p):
                dve.wait_ge(av_free.sem, av_free.next(4))
                nc.vector.reciprocal(sums[:, u], sums[:, u]).then_inc(own.sem, own.up())
                dve.wait_ge(own.sem, own.seen())
                o = outT[:, bass.ds(p, 1), :].rearrange("r o t -> r (o t)")
                return tt(o, o, sums[:, u], ALU.mult)

            def pair(u, p, following, further):
                if following:
                    rope(1, 0)
                    rope(1, 1)
                    qlo(1 - u)
                    maxima0()
                if further:
                    rope(0, 0)
                    rope(0, 1)
                if following:
                    divide(u, p).then_inc(own.sem, own.up())
                else:
                    divide(u, p).then_inc(outT_ready.sem, outT_ready.up())

            def finish1(n):
                dve.wait_ge(ms_dve.sem, ms_dve.next())
                o = ms3.rearrange("p i (g c) -> p i g c", g=GH)
                nc.vector.reciprocal(rinv, o[:, :, :, C1]).then_inc(own.sem, own.up())
                dve.wait_ge(own.sem, own.seen())
                tt(y[:, :, 32 * n:32 * n + 32].rearrange("p i (g c) -> p i g c", g=GH),
                   o[:, :, :, 0:C1], rinv.unsqueeze(3).broadcast_to([P, TILES, GH, C1]), ALU.mult).then_inc(ms_free.sem, ms_free.up())

            def maxima1():
                for column in range(GH * TILES):
                    for c in range(2):
                        row_max(c, column, c, CH, last=(column == GH * TILES - 1 and c == 1))
                tt(mx[:, 0], mx[:, 0], mx[:, 1], ALU.max).then_inc(ms_free.sem, ms_free.up())

            dve.wait_ge(sems["loaded"], 3 * DMAS)
            nc.vector.tensor_copy(ident_r[:], at["ident"])
            nc.vector.tensor_copy(mask_st[:], at["mask_st"])
            nc.vector.tensor_copy(mask_qk[:], at["mask_qk"])
            nc.vector.tensor_scalar(wf[:].rearrange("p n d -> p (n d)"), wfi, 1.0 / 127.0, None,
                                    ALU.mult).then_inc(sems["prep_done"], 1)
            both = at["bias1"].rearrange("p (n k) -> p n k", k=2)
            for k in range(2):
                whole, high_part = (a.rearrange("p (n k) -> p n k", k=2)[:, :, k] for a in (bias_whole, bias_high[:]))
                nc.vector.tensor_scalar(whole, both[:, :, k], at[("qb", "kb")[k]], (0.0, at["ke"])[k], ALU.mult,
                                        ALU.add).then_inc(sems["prep_done"], 1)
                nc.vector.tensor_scalar(high_part, both[:, :, k], at[("qc", "kc")[k]], None,
                                        ALU.mult).then_inc(sems["prep_done"], 1)
            dve.wait_ge(sems["prep_done"], 5)
            with repeat(dve, "batch", B, every) as b:
                dve.wait_ge(xb_loaded.sem, xb_loaded.next())
                normalise(TILES, lambda i: xb[:, i, :], lambda i: xn[:, i, :], xn_ready)
                for k in range(2):
                    for c in range(2):
                        rope(k, c)
                qlo(0)
                maxima0()
                rope(0, 0)
                rope(0, 1)
                with repeat(dve, "pairs", PAIRS // 2 - 1, every) as j:
                    for u in range(2):
                        pair(u, 2 * j + u, True, True)
                pair(0, PAIRS - 2, True, False)
                pair(1, PAIRS - 1, False, False)
                dve.wait_ge(ms_dve.sem, ms_dve.next())
                normalise(TILES, lambda i: ms3[:, i, :], lambda i: y[:, i, :])
                tt(xb[:], xb[:], y[:], ALU.add).then_inc(own.sem, own.up())
                dve.wait_ge(own.sem, own.seen())
                normalise(TILES, lambda i: xb[:, i, :], lambda i: xn[:, i, :], xn_ready)
                for f in range(FT):
                    for c in range(2):
                        dve.wait_ge(sg_ready.sem, sg_ready.next())
                        tt(hT[:, f, c * CH:(c + 1) * CH], sg, ms[:, CH:T], ALU.mult).then_inc(ms_free.sem, ms_free.up())
                dve.wait_ge(ms_dve.sem, ms_dve.next())
                normalise(TILES, lambda i: ms3[:, i, :], lambda i: y[:, i, :])
                tt(xb[:], xb[:], y[:], ALU.add).then_inc(own.sem, own.up())
                dve.wait_ge(own.sem, own.seen())
                normalise(TILES, lambda i: xb[:, i, :], lambda i: xn[:, i, :], xn_ready)
                dve.wait_ge(pool_prep.sem, pool_prep.next(2))
                dve.wait_ge(ms_dve.sem, ms_dve.next())
                tt(v1[:, :, :, 0:C1], ms3.rearrange("p i (h c) -> p i h c", h=H1),
                   over(at["bv1"], TILES).rearrange("p i (h c) -> p i h c", h=H1), ALU.add).then_inc(ms_free.sem, ms_free.up())
                maxima1()
                for n in range(GROUPS):
                    if n > 0:
                        finish1(n - 1)
                    if n < GROUPS - 1:
                        maxima1()
                finish1(GROUPS - 1)
                dve.wait_ge(ms_dve.sem, ms_dve.next())
                tt(y[:], ms3, over(at["bo1"], TILES), ALU.add).then_inc(own.sem, own.up())
                dve.wait_ge(own.sem, own.seen())
                tt(y[:], y[:], xn[:], ALU.add).then_inc(own.sem, own.up())
                dve.wait_ge(own.sem, own.seen())
                normalise(TILES, lambda i: y[:, i, :], lambda i: y[:, i, :])
                tt(x_all[:, bass.ds(b * TILES, TILES), :], xb[:], y[:], ALU.add).then_inc(batch_done.sem, batch_done.up())
            dve.wait_ge(sems["batch_done"], B + 1)

            def total(dst, a, axis="p s t h -> p s h t", op=ALU.add):
                return nc.vector.tensor_reduce(dst, a.rearrange(axis), AX.X, op)

            def per_tile(a):
                return a.unsqueeze(2).broadcast_to([P, B, EXPERTS])

            def first_largest(p, dst):
                nc.vector.tensor_reduce(gm[2], p, AX.X, ALU.max).then_inc(own.sem, own.up())
                dve.wait_ge(own.sem, own.seen())
                tt(gt[2], p, per_tile(gm[2]), ALU.is_ge).then_inc(own.sem, own.up())
                dve.wait_ge(own.sem, own.seen())
                tt(gt[2], gt[2], at["rank"].unsqueeze(1).broadcast_to([P, B, EXPERTS]), ALU.mult).then_inc(own.sem, own.up())
                dve.wait_ge(own.sem, own.seen())
                nc.vector.tensor_reduce(gm[3], gt[2], AX.X, ALU.max).then_inc(own.sem, own.up())
                dve.wait_ge(own.sem, own.seen())
                tt(dst, gt[2], per_tile(gm[3]), ALU.is_equal).then_inc(own.sem, own.up())
                dve.wait_ge(own.sem, own.seen())

            with repeat(dve, "tokens", TILES, every) as i:
                normalise(B, lambda s: x_all[:, bass.ds(s * TILES + i, 1), :].rearrange("p o d -> p (o d)"),
                          lambda s: xn[:, s, :], xn_ready)
                for half in range(2):
                    dve.wait_ge(ms_dve.sem, ms_dve.next())
                    done = tt(qkv[:, 2 * half:2 * half + 2, :],
                              ms[:].rearrange("p (r c) -> p r c", r=2)[:, :, 0:3 * D],
                              at["bin"].unsqueeze(1).broadcast_to([P, 2, 3 * D]), ALU.add)
                    if half == 0:
                        done.then_inc(ms_free.sem, ms_free.up())
                    else:
                        done.then_inc(own.sem, own.up())
                        dve.wait_ge(own.sem, own.seen())
                for s in range(B):
                    last = tt(prod[:, s], qkv[:, s, 0:D].unsqueeze(1).broadcast_to([P, B, D]),
                              qkv[:, :, D:2 * D], ALU.mult)
                last.then_inc(own.sem, own.up())
                dve.wait_ge(own.sem, own.seen())
                nc.vector.tensor_reduce(sc.rearrange("p s t h -> p (s t h)"),
                                        flat.rearrange("p (n c) -> p n c", c=C1), AX.X, ALU.add).then_inc(own.sem, own.up())
                dve.wait_ge(own.sem, own.seen())
                total(m2, sc, op=ALU.max).then_inc(own.sem, own.up())
                dve.wait_ge(own.sem, own.seen())
                tt(sc, sc, m2.unsqueeze(2).broadcast_to([P, B, B, H1]), ALU.subtract).then_inc(sc_ready.sem, sc_ready.up())
                dve.wait_ge(ex_ready.sem, ex_ready.next())
                total(sm2, ex).then_inc(own.sem, own.up())
                dve.wait_ge(own.sem, own.seen())
                nc.vector.reciprocal(sm2, sm2).then_inc(own.sem, own.up())
                dve.wait_ge(own.sem, own.seen())
                tt(ex, ex, sm2.unsqueeze(2).broadcast_to([P, B, B, H1]), ALU.mult).then_inc(own.sem, own.up())
                dve.wait_ge(own.sem, own.seen())
                for s in range(B):
                    last = tt(prod[:, s].rearrange("p t (h c) -> p t h c", h=H1),
                              ex[:, s].unsqueeze(3).broadcast_to([P, B, H1, C1]),
                              qkv[:, :, 2 * D:3 * D].rearrange("p t (h c) -> p t h c", h=H1), ALU.mult)
                last.then_inc(own.sem, own.up())
                dve.wait_ge(own.sem, own.seen())
                total(y[:, 0:B, :], prod, "p s t e -> p s e t").then_inc(tok_ready.sem, tok_ready.up())
                dve.wait_ge(ms_dve.sem, ms_dve.next())
                tt(y[:, 0:B, :], ms3[:, 0:B, :], over(at["bout"], B), ALU.add).then_inc(own.sem, own.up())
                dve.wait_ge(own.sem, own.seen())
                tt(y[:, 0:B, :], y[:, 0:B, :], xn[:, 0:B, :], ALU.add).then_inc(own.sem, own.up())
                dve.wait_ge(own.sem, own.seen())
                normalise(B, lambda s: y[:, s, :], lambda s: y[:, s, :])
                tt(y[:, 0:B, :], y[:, 0:B, :], over(at["ln1g"], B), ALU.mult).then_inc(own.sem, own.up())
                dve.wait_ge(own.sem, own.seen())
                tt(y[:, 0:B, :], y[:, 0:B, :], over(at["ln1b"], B), ALU.add).then_inc(xn_ready.sem, xn_ready.up())
                dve.wait_ge(xn_ready.sem, xn_ready.seen())
                nc.vector.tensor_copy(x1[:, bass.ds(i * B, B), :], y[:, 0:B, :]).then_inc(own.sem, own.up())
                dve.wait_ge(ms_dve.sem, ms_dve.next())
                tt(gt[0], ms[:, 0:B * EXPERTS].rearrange("p (s e) -> p s e", s=B),
                   at["bgate"].unsqueeze(1).broadcast_to([P, B, EXPERTS]), ALU.add).then_inc(own.sem, own.up())
                dve.wait_ge(own.sem, own.seen())
                nc.vector.tensor_reduce(gm[0], gt[0], AX.X, ALU.max).then_inc(own.sem, own.up())
                dve.wait_ge(own.sem, own.seen())
                tt(gt[0], gt[0], per_tile(gm[0]), ALU.subtract).then_inc(sc_ready.sem, sc_ready.up())
                dve.wait_ge(ex_ready.sem, ex_ready.next())
                nc.vector.tensor_reduce(gm[1], gt[1], AX.X, ALU.add).then_inc(own.sem, own.up())
                dve.wait_ge(own.sem, own.seen())
                nc.vector.reciprocal(gm[1], gm[1]).then_inc(own.sem, own.up())
                dve.wait_ge(own.sem, own.seen())
                tt(gt[1], gt[1], per_tile(gm[1]), ALU.mult).then_inc(own.sem, own.up())
                dve.wait_ge(own.sem, own.seen())
                first_largest(gt[1], gt[3])
                nc.vector.scalar_tensor_tensor(out=gt[4], in0=gt[3], scalar=-2.0, in1=gt[1],
                                               op0=ALU.mult, op1=ALU.add).then_inc(own.sem, own.up())
                dve.wait_ge(own.sem, own.seen())
                first_largest(gt[4], gt[5])
                tt(gt[6], gt[3], gt[5], ALU.add).then_inc(own.sem, own.up())
                dve.wait_ge(own.sem, own.seen())
                tt(gt[6], gt[6], gt[1], ALU.mult).then_inc(own.sem, own.up())
                dve.wait_ge(own.sem, own.seen())
                nc.vector.tensor_reduce(gm[4], gt[6], AX.X, ALU.add).then_inc(own.sem, own.up())
                dve.wait_ge(own.sem, own.seen())
                nc.vector.reciprocal(gm[4], gm[4]).then_inc(own.sem, own.up())
                dve.wait_ge(own.sem, own.seen())
                tt(gt[7], gt[6], per_tile(gm[4]), ALU.mult).then_inc(tok_ready.sem, tok_ready.up())
                dve.wait_ge(tok_ready.sem, tok_ready.seen())
                nc.vector.tensor_copy(comb[:, bass.ds(i * B, B), :], gt[7]).then_inc(own.sem, own.up())
                dve.wait_ge(ms_dve.sem, ms_dve.next())
                nc.vector.tensor_copy(acc[:, bass.ds(i * B, B), :], ms3[:, 0:B, :]).then_inc(own.sem, own.up())
                dve.wait_ge(own.sem, own.seen())

            combf = comb[:].rearrange("p n e -> p (n e)")
            accf = acc.rearrange("p n d -> p (n d)")
            with repeat(dve, "experts", EXPERTS // 2, every) as je:
                for e in range(2):
                    with repeat(dve, "chunks", TILES // 2, every) as j:
                        for u in range(2):
                            dve.wait_ge(y_full.sem, y_full.next())
                            for s in range(B):
                                tile = (2 * j + u) * B + s
                                a = accf[:, bass.ds(tile * D, D)]
                                last = nc.vector.scalar_tensor_tensor(
                                    out=a, in0=av[:, u * CH + s * D:u * CH + (s + 1) * D],
                                    scalar=combf[:, bass.ds(tile * EXPERTS + 2 * je + e, 1)],
                                    in1=a, op0=ALU.mult, op1=ALU.add)
                            last.then_inc(y_used.sem, y_used.up())
                            dve.wait_ge(y_used.sem, y_used.seen())

            with repeat(dve, "last", TILES // 2, every) as j:
                for u in range(2):
                    i = 2 * j + u
                    tt(y[:, 0:B, :], x1[:, bass.ds(i * B, B), :], acc[:, bass.ds(i * B, B), :], ALU.add).then_inc(own.sem, own.up())
                    dve.wait_ge(own.sem, own.seen())
                    normalise(B, lambda s: y[:, s, :], lambda s: y[:, s, :])
                    tt(y[:, 0:B, :], y[:, 0:B, :], over(at["ln2g"], B), ALU.mult).then_inc(own.sem, own.up())
                    dve.wait_ge(own.sem, own.seen())
                    tt(y[:, 0:B, :], y[:, 0:B, :], over(at["ln2b"], B), ALU.add).then_inc(own.sem, own.up())
                    dve.wait_ge(own.sem, own.seen())
                    normalise(B, lambda s: y[:, s, :], lambda s: y[:, s, :])
                    dve.wait_ge(stored[u].sem, stored[u].next())
                    tt(ocur[:, u], xs[:, :, bass.ds(i, 1), :].rearrange("p s o d -> p s (o d)"),
                       y[:, 0:B, :], ALU.add).then_inc(o_ready.sem, o_ready.up())
                    dve.wait_ge(o_ready.sem, o_ready.seen())


def kernel(**inputs):
    import numpy as np
    import concourse.bacc as bacc
    from concourse.bass_utils import run_bass_kernel_spmd

    f32 = np.float32
    g = {k: np.asarray(v) for k, v in inputs.items()}

    def row(v):
        return np.broadcast_to(v.reshape(1, -1), (P, v.size))

    x_in = np.ascontiguousarray(g["L0_attn_x"].reshape(B * TILES, P, D).transpose(1, 0, 2).reshape(P, -1))
    swap = np.arange(P) // C0 * C0 + (np.arange(P) % C0 + C0 // 2) % C0
    wl0 = np.empty((PAIRS, P, 5, P), f32)
    for k, name in enumerate(("wq", "wk", "wv")):
        w = g[f"L0_attn_{name}"].reshape(PAIRS, P, D).transpose(0, 2, 1)
        wl0[:, :, 2 * k, :] = w
        if k < 2:
            wl0[:, :, 2 * k + 1, :] = w[:, :, swap]
    wl0 = wl0.reshape(PAIRS, P, WL0)
    inv = (1.0 / 10000.0 ** (np.arange(0, C0, 2, dtype=f32) / f32(C0))).astype(f32)
    angle = np.outer(np.arange(T, dtype=f32), inv).astype(f32).T[np.arange(P) % (C0 // 2)]
    sign = np.where(np.arange(P) % C0 < C0 // 2, -1.0, 1.0).astype(f32)[:, None]
    rope = np.concatenate([np.cos(angle), sign * np.sin(angle)], axis=1).astype(f32)
    wffn = np.concatenate([g["L0_ffn_w_gate"].T, g["L0_ffn_w_up"].T,
                           g["L0_ffn_w_down"].T.reshape(FT, P, D).transpose(1, 0, 2).reshape(P, -1)], axis=1)
    wmoe = np.concatenate([g["L1_ffn_w1"].transpose(0, 2, 1),
                           g["L1_ffn_w2"].transpose(0, 2, 1).reshape(EXPERTS, HID // P, P, D)
                           .transpose(0, 2, 1, 3).reshape(EXPERTS, P, -1),
                           g["L1_ffn_b1"].reshape(EXPERTS, HID // P, P).transpose(0, 2, 1)], axis=2)
    r = np.arange(P)
    dims = [(GH * n + r // 32) * C1 + r % C1 for n in range(GROUPS)]
    wqkv, bqkv = g["L1_attn_w_qkv"], g["L1_attn_b_qkv"]
    j = r % 32 // C1
    one = (r % 32 == 3 * C1)
    parts = {
        "wqk1": np.concatenate([wqkv[k * D + d].T for d in dims for k in range(2)], axis=1),
        "bias1": np.stack([bqkv[k * D + d] for d in dims for k in range(2)], axis=1),
        "qb": j == 2, "qc": 1.0 * (j < 2) - 1.0 * (j == 2),
        "kb": j == 1, "kc": 1.0 * ((j == 0) | (j == 2)) - 1.0 * (j == 1), "ke": one,
        "ident": np.eye(P), "mask_qk": np.where(r[:, None] >= r, 0.0, MASKED),
        "mask_st": np.where(r[:, None] <= r, 0.0, MASKED),
        "wo0": g["L0_attn_wo"].T.reshape(PAIRS, P, D).transpose(1, 0, 2).reshape(P, -1),
        "wv1": wqkv[2 * D:].T, "wo1": g["L1_attn_w_o"].T, "win": g["L1_ffn_in_proj_w"].T,
        "wout": g["L1_ffn_out_w"].T, "wgate": g["L1_ffn_gate_w"].T, "bv1": row(bqkv[2 * D:]),
        "bo1": row(g["L1_attn_b_o"]), "bin": row(g["L1_ffn_in_proj_b"]), "bout": row(g["L1_ffn_out_b"]),
        "bgate": row(g["L1_ffn_gate_b"]), "ln1g": row(g["L1_ffn_ln1_g"]), "ln1b": row(g["L1_ffn_ln1_b"]),
        "ln2g": row(g["L1_ffn_ln2_g"]), "ln2b": row(g["L1_ffn_ln2_b"]),
        "rank": row(np.arange(EXPERTS, 0, -1)), "b2": np.tile(g["L1_ffn_b2"], (P // EXPERTS, 1)),
    }
    pack = np.concatenate([np.asarray(parts[n], f32).reshape(P, w) for n, w in PACK], axis=1)
    arrays = {"x_in": x_in, "pack": pack, "rope": rope, "wl0": wl0, "wffn": wffn, "wmoe": wmoe}
    arrays = {n: np.ascontiguousarray(a) for n, a in arrays.items()}

    nc = bacc.Bacc("TRN2", target_bir_lowering=False, num_devices=1)
    aps = [nc.dram_tensor(n, a.shape, mybir.dt.from_np(a.dtype), kind="ExternalInput").ap()
           for n, a in arrays.items()]
    out = nc.dram_tensor("out", (TILES, P, B * D), F32, kind="ExternalOutput").ap()
    block_program(nc, *aps, out)
    result = run_bass_kernel_spmd(nc, [arrays], core_ids=[0]).results[0]["out"]
    return result.reshape(TILES, P, B, D).transpose(2, 0, 1, 3).reshape(B, T, D)
```

```python
from contextlib import ExitStack, contextmanager

import concourse.bass as bass
from concourse import mybir

F32 = mybir.dt.float32
F32R = mybir.dt.float32r
I32 = mybir.dt.int32
ACT = mybir.ActivationFunctionType
ALU = mybir.AluOpType
AX = mybir.AxisListType

P = 128
B, T, D = 4, 1024, 128
TILES = T // P
CH = 512
H0, C0 = 16, 64
PAIRS = H0 // 2
FFN = 384
FT = FFN // P
H1, C1 = 16, 8
GROUPS, GH = 4, 4
EXPERTS, HID = 8, 512
EPS = 1e-5
SCALE0 = C0 ** -0.5
SCALE1 = D ** -0.5
SCALE2 = C1 ** -0.5
MASKED = -1e30

PACK = [
    ("wqk1", 2 * GROUPS * P), ("ident", P), ("mask_st", P), ("mask_qk", P), ("wo0", PAIRS * D),
    ("wv1", D), ("wo1", D),
    ("win", 3 * D), ("wout", D), ("wgate", EXPERTS), ("bv1", D), ("bo1", D), ("bin", 3 * D), ("bout", D),
    ("bgate", EXPERTS), ("ln1g", D), ("ln1b", D), ("ln2g", D), ("ln2b", D), ("rank", EXPERTS),
    ("qb", 1), ("qc", 1), ("kb", 1), ("kc", 1), ("ke", 1), ("bias1", 2 * GROUPS), ("b2", D),
]
WL0 = 5 * P
WE = HID + HID // P * D + HID // P

PER = {
    "batch": {
        "av1_free": 4, "av_free": 32, "av_full": 36, "batch_done": 1, "dve_own": 80, "hi1_done": 8,
        "hi_done": 64, "klo_done": 16, "ms_act": 38, "ms_dve": 402, "ms_free": 383, "outT_ready": 2,
        "p_ready": 256, "p_used": 140, "pool_own": 17, "pool_prep": 2, "qlo_done": 16, "rope_done": 32,
        "rows0_loaded": 256, "rows1_loaded": 256, "rows_ready": 12, "rstd_ready": 6, "sg_ready": 6,
        "st_full": 256, "stack_done": 20, "var_ready": 6, "w0_loaded": 128, "wide_free": 48,
        "wide_full": 48, "x_loaded": 16, "xn_ready": 3,
    },
    "pairs": {
        "av_free": 8, "av_full": 8, "dve_own": 14, "hi_done": 16, "klo_done": 4, "ms_act": 4,
        "ms_dve": 56, "ms_free": 50, "p_ready": 32, "p_used": 28, "qlo_done": 4, "rope_done": 8,
        "rows0_loaded": 64, "rows_ready": 2, "st_full": 32, "w0_loaded": 32,
    },
    "chunks": {
        "dve_own": 46, "ex_ready": 2, "h_full": 32, "ms_act": 4, "ms_dve": 5, "ms_free": 6, "o_ready": 1,
        "relu_done": 32, "rstd_ready": 4, "sc_ready": 2, "stored": 16, "tok_ready": 2, "var_ready": 4,
        "xn_ready": 2, "y_full": 8, "y_used": 8,
    },
}


class Tally:

    def __init__(self, name, sem, start=0, step=1):
        self.name, self.sem, self.turn, self.n, self.step, self.total = name, sem, start, 0, step, 0

    def value(self):
        return self.turn + self.n

    def count(self, k=1):
        self.n += k * self.step
        self.total += k * self.step

    def up(self):
        self.count()
        return self.step

    def next(self, k=1):
        self.count(k)
        return self.value()

    def seen(self, more=0):
        return self.value() + more


class Signal:

    def __init__(self, sem, step):
        self.sem, self.step = sem, step

    def up(self):
        return self.step


@contextmanager
def repeat(engine, name, count, tallies):
    before = [(t, t.value(), t.total) for t in tallies]
    per = PER[name]
    with engine.Fori(0, count) as i:
        for t in tallies:
            t.turn, t.n, t.total = t.value() + i * per.get(t.name, 0) if per.get(t.name, 0) else t.value(), 0, 0
        yield i
        for t in tallies:
            assert t.total == per.get(t.name, 0), (name, t.name, t.total)
    for t, value, total in before:
        t.turn, t.n, t.total = value + count * per.get(t.name, 0), 0, total + count * per.get(t.name, 0)


def block_program(nc, x_in, pack, rope, wl0, wffn, wmoe, out):
    with ExitStack() as ctx:
        def sb(name, shape, dt=F32):
            return ctx.enter_context(nc.sbuf_tensor(name, shape, dt))

        sems = {}

        def sem(name):
            sems[name] = ctx.enter_context(nc.semaphore(name))

        x_all = sb("x_all", [P, B * TILES, D])
        cst = sb("cst", [P, sum(w for _, w in PACK)])
        at = {}
        col = 0
        for name, w in PACK:
            at[name] = cst[:, col:col + w]
            col += w
        ident_r = sb("ident_r", [P, P], F32R)
        mask_st = sb("mask_st_r", [P, P], F32R)
        mask_qk = sb("mask_qk_r", [P, P], F32R)
        wf = sb("wf", [P, 3 * FT, D])
        w0 = sb("w0", [P, 5, P])
        neghalf = sb("neghalf", [P, 1])
        stats = sb("stats", [P, TILES, 6])
        mv = sb("mv", [P, TILES, 2])
        var = sb("var", [P, TILES])
        rstd = sb("rstd", [P, TILES])
        mx = sb("mx", [P, 2, GH * TILES])
        mrows = sb("mrows", [GH * TILES, P], F32R)
        xb = sb("xb", [P, TILES, D])
        xn = sb("xn", [P, TILES, D])
        xT = sb("xT", [P, T])
        y = sb("y", [P, TILES, D])

        parts = sb("parts", [P, 16, T], F32R)
        ops0 = parts[:].rearrange("p (u k h) t -> p u k h t", u=2, k=4)
        QA, QB, KA, KB = 0, 1, 2, 3
        ops1 = parts[:, 0:10].rearrange("p (u k) t -> p u k t", u=2)

        big = sb("big", [P, 8, T])
        outT = big
        hT = big
        p1 = big[:].rearrange("p (u g) t -> p u g t", u=2)

        vals = sb("vals", [P, 4, T])
        v0 = vals[:].rearrange("p (u k) (t c) -> p u (k t) c", u=2, c=2 * P)
        v0 = v0.rearrange("p u t (h c) -> p u t h c", h=2)
        v1 = vals[:].rearrange("p k (t h c) -> p (k t) h c", t=2, c=32)

        p0 = sb("p0", [P, 2, T])
        tabs = sb("tabs", [P, 2 * T + 2 * GROUPS])
        cosT, sinT = tabs[:, 0:T], tabs[:, T:2 * T]

        scr = sb("scr", [P, 5, T])
        qs, ks = scr[:, 0], scr[:, 1]
        t1, t2 = scr[:, 2, 0:CH], scr[:, 2, CH:T]
        sums = scr[:, 3:5]
        xq, xk, hq, hk = scr[:, 0], scr[:, 1], scr[:, 2], scr[:, 3]
        coming = p0[:, 1].rearrange("p (n d) -> p n d", d=D)
        coming_norm = scr[:, 4].rearrange("p (n d) -> p n d", d=D)
        wfi = scr[:, 0:2].rearrange("p a t -> p (a t)")[:, 0:3 * FT * D].bitcast(I32)
        sg = [scr[:, 0, 0:CH], scr[:, 0, CH:T], scr[:, 1, 0:CH]]
        bigf, valsf = big[:].rearrange("p n t -> p (n t)"), vals[:].rearrange("p n t -> p (n t)")
        we = [bigf[:, e * WE:(e + 1) * WE] for e in range(EXPERTS - 1)] + [valsf[:, 0:WE]]
        x1, x1T, acc = (valsf[:, T + k * CH:T + (k + 1) * CH] for k in range(1, 4))
        halves = [tabs[:, f * CH:(f + 1) * CH] for f in range(4)] + [xT[:, CH:T], p0[:, 1, CH:T]]
        halves += [a[:, 4:8, :].rearrange("p n d -> p (n d)") for a in (xn, y)]
        relu = [halves[0:4], halves[4:8]]
        result = w0[:].rearrange("p k c -> p (k c)")[:, 0:B * D]
        qkv = scr[:, 0:2].rearrange("p a t -> p (a t)")[:, 0:B * 3 * D].rearrange("p (s c) -> p s c", s=B)
        flat = scr[:, 2:4].rearrange("p a t -> p (a t)")
        prod = scr[:, 2:4].rearrange("p a (b t c) -> p (a b) t c", b=2, c=D)
        sc = scr[:, 4, 0:256].rearrange("p (s t h) -> p s t h", s=B, t=B)
        ex = scr[:, 4, 256:512].rearrange("p (s t h) -> p s t h", s=B, t=B)
        m2 = scr[:, 4, 512:576].rearrange("p (s h) -> p s h", s=B)
        sm2 = scr[:, 4, 576:640].rearrange("p (s h) -> p s h", s=B)
        gt = [scr[:, 4, 640 + 32 * k:672 + 32 * k].rearrange("p (s e) -> p s e", s=B) for k in range(8)]
        gm = [scr[:, 4, 896 + 4 * k:900 + 4 * k] for k in range(8)]
        cT, cbT = p0[:, 0, 0:CH], p0[:, 0, CH:T]
        sT = p0[:, 1, 0:CH]
        xs = x_all[:].rearrange("p (s i) d -> p s i d", s=B)
        rinv = stats[:].rearrange("p i s -> p (i s)")[:, 0:TILES * GH].rearrange("p (i g) -> p i g", g=GH)
        bias_whole = tabs[:, 2 * T:2 * T + 2 * GROUPS]
        bias_high = sb("bias_high", [P, 2 * GROUPS])
        comb = xb[:, 0:2, :].rearrange("p a (n e) -> p (a n) e", e=EXPERTS)

        st = ctx.enter_context(nc.psum_tensor("st", [P, 2, T], F32))
        av = ctx.enter_context(nc.psum_tensor("av", [P, T], F32))
        ms = ctx.enter_context(nc.psum_tensor("ms", [P, T], F32))
        ms3 = ms[:].rearrange("p (n d) -> p n d", d=D)
        wide = [ms, st[:, 0], st[:, 1]]

        for name in (
            "loaded", "x_loaded", "w0_loaded", "rows0_loaded", "rows1_loaded", "we_loaded", "stored",
            "dve_own", "act_own", "pool_own",
            "prep_done", "pool_prep",
            "var_ready", "rstd_ready", "xn_ready",
            "ms_dve", "ms_act", "ms_free",
            "st_full", "p_ready", "p_used",
            "av_full", "av_free", "av1_free",
            "rope_done", "hi_done", "qlo_done", "klo_done", "rows_ready", "outT_ready",
            "wide_full", "wide_free", "apart",
            "hi1_done", "stack_done",
            "sg_ready", "tok_ready", "sc_ready", "ex_ready", "batch_done",
            "h_full", "relu_done", "y_full", "y_used", "o_ready",
        ):
            sem(name)

        def tally(name, start=0, step=1):
            return Tally(name, sems[name], start, step)

        def signal(name, step=1):
            return Signal(sems[name], step)

        def tile0(m):
            part, m = divmod(m, TILES)
            h, j = divmod(m, TILES // 2)
            return h, TILES - 1 - j - part * TILES // 2

        DMAS = 16

        def apart(engine):
            engine.sem_inc(sems["apart"], 1)

        block = ctx.enter_context(nc.Block())

        @block.sync
        def _(sp):
            loaded, x_loaded = signal("loaded", step=DMAS), signal("x_loaded", step=DMAS)
            w0_loaded = tally("w0_loaded", step=DMAS)
            rows0, rows1 = signal("rows0_loaded", step=DMAS), signal("rows1_loaded", step=DMAS)
            we_loaded, stored = signal("we_loaded", step=DMAS), tally("stored", DMAS, DMAS)
            hi_done, rows_ready = tally("hi_done"), tally("rows_ready")
            o_ready = tally("o_ready")
            pool_prep, outT_ready = tally("pool_prep"), tally("outT_ready")
            every = [outT_ready, w0_loaded, stored, hi_done,
                     rows_ready, o_ready, pool_prep]

            def max_rows0(u):
                sp.wait_ge(rows_ready.sem, rows_ready.next())
                sp.dma_start(ops0[64:65, u, QB, 0, :].bitcast(F32), mrows[0:TILES, :].bitcast(F32)).then_inc(
                    rows0.sem, rows0.up())
                sp.dma_start(ops0[0:1, u, QB, 1, :].bitcast(F32),
                             mrows[TILES:2 * TILES, :].bitcast(F32)).then_inc(rows0.sem, rows0.up())

            def load_w0(p):
                sp.dma_start(w0[:].rearrange("p k c -> p (k c)"),
                             wl0[bass.ds(p, 1)].rearrange("o p c -> (o p) c")).then_inc(
                                 w0_loaded.sem, w0_loaded.up())

            def max_rows1(u):
                sp.wait_ge(rows_ready.sem, rows_ready.next())
                for g in range(GH):
                    r = 32 * g + 24
                    sp.dma_start(ops1[r:r + 1, u, GH, :].bitcast(F32),
                                 mrows[TILES * g:TILES * (g + 1), :].bitcast(F32)).then_inc(rows1.sem, rows1.up())

            sp.dma_start(cst[:], pack).then_inc(loaded.sem, loaded.up())
            sp.dma_start(tabs[:, 0:2 * T], rope).then_inc(loaded.sem, loaded.up())
            sp.dma_start(wfi, wffn).then_inc(loaded.sem, loaded.up())
            sp.dma_start(p0[:, 1], x_in[:, 0:TILES * D]).then_inc(x_loaded.sem, x_loaded.up())
            load_w0(0)
            with repeat(sp, "batch", B, every) as b:
                sp.wait_ge(hi_done.sem, hi_done.next(8))
                load_w0(1)
                sp.wait_ge(pool_prep.sem, pool_prep.next())
                max_rows0(0)
                with repeat(sp, "pairs", PAIRS // 2 - 1, every) as j:
                    for u in (1, 0):
                        sp.wait_ge(hi_done.sem, hi_done.next(8))
                        load_w0(2 * j + 3 - u)
                        max_rows0(u)
                max_rows0(1)
                hi_done.count(8)
                sp.wait_ge(outT_ready.sem, outT_ready.next(2))
                sp.dma_start(p0[:, 1], x_in[:, bass.ds((b + 1) * TILES * D, TILES * D)]).then_inc(x_loaded.sem,
                                                                                               x_loaded.up())
                load_w0(0)
                pool_prep.count()
                for n in range(GROUPS):
                    max_rows1(n % 2)
            sp.wait_ge(sems["batch_done"], B + 1)
            sp.wait_ge(w0_loaded.sem, w0_loaded.seen())
            sp.sem_inc(sems["stored"], DMAS)
            for e in range(EXPERTS):
                sp.dma_start(we[e], wmoe[e]).then_inc(we_loaded.sem, we_loaded.up())
            with repeat(sp, "chunks", TILES - 1, every) as j:
                sp.wait_ge(o_ready.sem, o_ready.next())
                sp.dma_start(out[bass.ds(j, 1)].rearrange("o p c -> (o p) c"), result).then_inc(
                    stored.sem, stored.up())
            sp.wait_ge(o_ready.sem, o_ready.next())
            sp.dma_start(out[TILES - 1], result).then_inc(stored.sem, stored.up())
            sp.wait_ge(stored.sem, stored.seen())

        @block.tensor
        def _(pe):
            ms_free, ms_dve, ms_act = tally("ms_free"), signal("ms_dve"), signal("ms_act")
            xn_ready = tally("xn_ready")
            w0_loaded = tally("w0_loaded", step=DMAS)
            rows0, rows1 = tally("rows0_loaded", step=DMAS), tally("rows1_loaded", step=DMAS)
            st_full, st_free, p_ready, p_used = (
                signal("st_full"), tally("p_ready"), tally("p_ready", start=2), signal("p_used"))
            av_full, av_free, av1_free = signal("av_full"), tally("av_free"), tally("av1_free")
            wide_full, wide_free = signal("wide_full"), tally("wide_free")
            hi_done, qlo_done, klo_done = tally("hi_done"), tally("qlo_done"), tally("klo_done")
            rope_done = tally("rope_done")
            rows_ready, stack_done, hi1_done = tally("rows_ready"), tally("stack_done"), tally("hi1_done")
            outT_ready, tok_ready, pool_prep = tally("outT_ready"), tally("tok_ready"), tally("pool_prep")
            h_full, relu_done, relu_free = tally("h_full"), tally("relu_done", start=4), tally("relu_done")
            y_full, y_free = signal("y_full"), tally("y_used")
            every = [ms_free, xn_ready, w0_loaded, rows0, rows1, st_free,
                     p_ready, av_free, av1_free, wide_free, hi_done, qlo_done, klo_done, rows_ready, stack_done,
                     rope_done, hi1_done, outT_ready, tok_ready, pool_prep, h_full, relu_done, relu_free, y_free,
                     ]
            pe.sem_inc(sems["p_used"], 1)

            def transposed(source, n):
                pe.wait_ge(ms_free.sem, ms_free.next())
                for i in range(n):
                    mm = nc.tensor.transpose(ms3[:, i, :], source(i), at["ident"])
                mm.then_inc(ms_act.sem, ms_act.up())

            def project0(k, c, to=ms):
                if k == 0 and c == 0:
                    pe.wait_ge(w0_loaded.sem, w0_loaded.next())
                    pe.wait_ge(ms_free.sem, ms_free.seen(1))
                for r in range(2):
                    mm = nc.tensor.matmul(to[:, r * CH:(r + 1) * CH], w0[:, k + r, :],
                                          xT[:, c * CH:(c + 1) * CH], start=True, stop=True)
                mm.then_inc(ms_dve.sem, ms_dve.up())

            def coming_q():
                project0(0, 0)
                pe.wait_ge(av_free.sem, av_free.seen(2))
                project0(0, 1, av)

            def values0(chunks_out=1):
                pe.wait_ge(rope_done.sem, rope_done.next(chunks_out))
                pe.wait_ge(ms_free.sem, ms_free.next())
                for i in range(TILES):
                    mm = nc.tensor.matmul(ms3[:, i, :], xT[:, i * P:(i + 1) * P], w0[:, 4, :],
                                          start=True, stop=True)
                mm.then_inc(ms_act.sem, ms_act.up())

            def scores_qk0(u, m):
                h, i = tile0(m)
                if m == 0:
                    pe.wait_ge(hi_done.sem, hi_done.next(6))
                    pe.wait_ge(qlo_done.sem, qlo_done.next(2))
                if m == TILES // 2:
                    pe.wait_ge(hi_done.sem, hi_done.next(2))
                for c in range(i // 4 + 1):
                    pe.wait_ge(ms_free.sem, ms_free.next() - (0 if m == 0 and c == 0 else 1))
                    half = (c if i >= 4 else (3 - i) % 2) * CH
                    diagonal = c == i // 4
                    n = (i % 4 + 1) * P if diagonal else CH
                    mm = nc.tensor.matmul(ms[:, half:half + n], ops0[:, u, QA, h, i * P:(i + 1) * P],
                                          ops0[:, u, KA, h, c * CH:c * CH + n], start=True, stop=True)
                    if diagonal:
                        mm = nc.tensor.matmul(ms[:, half + n - P:half + n], ident_r[:], mask_qk[:], start=False,
                                              stop=True, skip_group_check=True)
                    mm.then_inc(ms_dve.sem, ms_dve.up())

            def scores_wide0(m):
                h, i = tile0(m)
                to = wide[m % 3]
                if m == 0:
                    pe.wait_ge(hi_done.sem, hi_done.next(8))
                    pe.wait_ge(qlo_done.sem, qlo_done.next(2))
                    pe.wait_ge(ms_free.sem, ms_free.seen(1))
                if m >= 3:
                    pe.wait_ge(wide_free.sem, wide_free.next())
                for c in range(i // 4 + 1):
                    end = min((c + 1) * CH, (i + 1) * P)
                    nc.tensor.matmul(to[:, c * CH:end], ops0[:, 0, QA, h, i * P:(i + 1) * P],
                                     ops0[:, 0, KA, h, c * CH:end], start=True, stop=True)
                nc.tensor.matmul(to[:, i * P:(i + 1) * P], ident_r[:], mask_qk[:], start=False, stop=True,
                                 skip_group_check=True).then_inc(wide_full.sem, wide_full.up())

            def maxima(n):
                pe.wait_ge(ms_free.sem, ms_free.seen(1))
                mm = nc.tensor.transpose(ms[0:n, 0:P], mx[:, 0, 0:n], at["ident"])
                mm.then_inc(ms_act.sem, ms_act.up())
                pe.wait_ge(rows_ready.sem, rows_ready.next())

            def chunks(kt):
                return [(max(c * CH, kt * P), (c + 1) * CH) for c in range(kt // 4, 2)]

            def scores_st0(u, h, kt):
                pe.wait_ge(st_free.sem, st_free.next())
                for a, z in chunks(kt):
                    diagonal = a == kt * P
                    nc.tensor.matmul(st[:, kt % 2, a:z], ops0[:, u, KA, h, kt * P:(kt + 1) * P],
                                     ops0[:, u, QA, h, a:z], start=True, stop=False)
                    mm = nc.tensor.matmul(st[:, kt % 2, a:z], ops0[:, u, KB, h, kt * P:(kt + 1) * P],
                                          ops0[:, u, QB, h, a:z], start=False, stop=True)
                    if diagonal:
                        mm = nc.tensor.matmul(st[:, kt % 2, a:a + P], ident_r[:], mask_st[:], start=False,
                                              stop=True, skip_group_check=True)
                mm.then_inc(st_full.sem, st_full.up())

            def weigh0(u, h, kt):
                pe.wait_ge(p_ready.sem, p_ready.next())
                for a, z in chunks(kt):
                    if kt == 0:
                        pe.wait_ge(av_free.sem, av_free.next())
                    last = kt == z // P - 1
                    mm = nc.tensor.matmul(av[:, a:z], v0[:, u, kt, h, :], p0[:, kt % 2, a:z],
                                          start=(kt == 0), stop=last)
                    if last:
                        mm.then_inc(av_full.sem, av_full.up())
                if kt < TILES - 1:
                    mm.then_inc(p_used.sem, p_used.up())

            def pair(u, following, further):
                pe.wait_ge(klo_done.sem, klo_done.next(2))
                pe.wait_ge(rows0.sem, rows0.next(2))
                scores_st0(u, 0, 0)
                for s in range(2 * TILES):
                    if s + 1 < 2 * TILES:
                        scores_st0(u, *divmod(s + 1, TILES))
                    if following and s >= TILES:
                        scores_qk0(1 - u, 2 * (s - TILES))
                    if following and s == 0:
                        pe.wait_ge(rope_done.sem, rope_done.next(2))
                    weigh0(u, *divmod(s, TILES))
                    if following:
                        if s == 1:
                            project0(2, 0)
                        if s == 3:
                            pe.wait_ge(rope_done.sem, rope_done.next())
                            project0(2, 1)
                        if s == 5:
                            values0()
                        if s >= TILES:
                            scores_qk0(1 - u, 2 * (s - TILES) + 1)
                if following:
                    maxima(2 * TILES)
                if further:
                    coming_q()

            def project1(n, k, to=ms):
                if to is ms:
                    pe.wait_ge(ms_free.sem, ms_free.seen(1))
                w = at["wqk1"][:, (2 * n + k) * P:(2 * n + k + 1) * P]
                for c in range(2):
                    mm = nc.tensor.matmul(to[:, c * CH:(c + 1) * CH], w, xT[:, c * CH:(c + 1) * CH],
                                          start=True, stop=True)
                mm.then_inc(ms_act.sem, ms_act.up())

            def scores_qk1(u, m, c):
                g, i = divmod(m, TILES)
                if c == 0 and m == 0:
                    pe.wait_ge(stack_done.sem, stack_done.next())
                if c == 0 and i == 0:
                    pe.wait_ge(stack_done.sem, stack_done.next())
                pe.wait_ge(ms_free.sem, ms_free.next() - (0 if m == 0 and c == 0 else 1))
                nc.tensor.matmul(ms[:, c * CH:(c + 1) * CH], ops1[:, u, GH, i * P:(i + 1) * P],
                                 ops1[:, u, g, c * CH:(c + 1) * CH], start=True,
                                 stop=True).then_inc(ms_dve.sem, ms_dve.up())

            def scores_st1(u, kt, g):
                pe.wait_ge(st_free.sem, st_free.next())
                for c in range(2):
                    mm = nc.tensor.matmul(st[:, g % 2, c * CH:(c + 1) * CH],
                                          ops1[:, u, g, kt * P:(kt + 1) * P],
                                          ops1[:, u, GH, c * CH:(c + 1) * CH], start=True, stop=True)
                mm.then_inc(st_full.sem, st_full.up())

            def weigh1(head, kt, c):
                if c == 0:
                    pe.wait_ge(p_ready.sem, p_ready.next(GH))
                for g in range(GH):
                    mm = nc.tensor.matmul(av[32 * g:32 * g + 32, c * CH:(c + 1) * CH],
                                          v1[:, kt, head + g, :], p1[:, kt % 2, g, c * CH:(c + 1) * CH],
                                          start=(kt == 0), stop=(kt == TILES - 1), skip_group_check=True)
                if c == 1:
                    if kt == TILES - 1:
                        mm.then_inc(av_full.sem, av_full.up())
                    else:
                        mm.then_inc(p_used.sem, p_used.up())

            def finish1():
                pe.wait_ge(ms_free.sem, ms_free.next())
                for i in range(TILES):
                    mm = nc.tensor.transpose(ms3[:, i, :], p0[:, 0, i * P:(i + 1) * P], at["ident"])
                mm.then_inc(ms_dve.sem, ms_dve.up())

            def group(n):
                u, following = n % 2, n < GROUPS - 1
                if following:
                    project1(n + 1, 0)
                    project1(n + 1, 1, wide[2])
                pe.wait_ge(rows1.sem, rows1.next(GH))
                scores_st1(u, 0, 0)
                for s in range(GH * TILES):
                    kt, g = divmod(s + 1, GH)
                    tile = 2 * (s - GH - 1) if s < 2 * (GH + 1) else s
                    if following and s > GH:
                        scores_qk1(1 - u, tile, 0)
                    if s == 0 and following:
                        pe.wait_ge(hi1_done.sem, hi1_done.next(2))
                    if kt < TILES:
                        scores_st1(u, kt, g)
                    if following and GH < s < 2 * (GH + 1):
                        scores_qk1(1 - u, tile, 1)
                        tile += 1
                        scores_qk1(1 - u, tile, 0)
                    if s % GH in (1, 2) and s > GH:
                        weigh1(n * GH, s // GH - 1, s % GH - 1)
                    if s == GH and n > 0:
                        pe.wait_ge(av1_free.sem, av1_free.next())
                        finish1()
                    if following and s > GH:
                        scores_qk1(1 - u, tile, 1)
                for c in range(2):
                    weigh1(n * GH, TILES - 1, c)
                if following:
                    maxima(GH * TILES)

            pe.wait_ge(sems["loaded"], 3 * DMAS)
            pe.wait_ge(sems["prep_done"], 5)
            with repeat(pe, "batch", B, every):
                pe.wait_ge(xn_ready.sem, xn_ready.next())
                transposed(lambda i: coming_norm[:, i, :], TILES)
                project0(0, 0)
                project0(0, 1, wide[1])
                project0(2, 0, wide[2])
                pe.wait_ge(rope_done.sem, rope_done.next())
                project0(2, 1)
                values0(3)
                for m in range(2 * TILES):
                    scores_wide0(m)
                pe.wait_ge(wide_free.sem, wide_free.next(3))
                maxima(2 * TILES)
                coming_q()
                pe.wait_ge(pool_prep.sem, pool_prep.next())
                apart(pe)
                with repeat(pe, "pairs", PAIRS // 2 - 1, every):
                    for u in range(2):
                        pair(u, True, True)
                pair(0, True, False)
                pair(1, False, False)
                pe.wait_ge(ms_free.sem, ms_free.seen(1))
                for p in range(PAIRS):
                    if p == 0 or p == PAIRS - 1:
                        pe.wait_ge(outT_ready.sem, outT_ready.next())
                    for i in range(TILES):
                        mm = nc.tensor.matmul(ms3[:, i, :], outT[:, p, i * P:(i + 1) * P],
                                              at["wo0"][:, p * D:(p + 1) * D], start=(p == 0 and i % 4 == 0),
                                              stop=(p == PAIRS - 1), skip_group_check=True)
                        if p == PAIRS - 1 and i == TILES // 2 - 1:
                            mm.then_inc(ms_dve.sem, ms_dve.up())
                mm.then_inc(ms_dve.sem, ms_dve.up())
                pe.wait_ge(xn_ready.sem, xn_ready.next())
                transposed(lambda i: xn[:, i, :], TILES)
                for k in range(2 * FT):
                    f, c = divmod(k, 2)
                    pe.wait_ge(ms_free.sem, ms_free.next() - min(k, 2))
                    for r in range(2):
                        mm = nc.tensor.matmul(wide[k % 3][:, r * CH:(r + 1) * CH], wf[:, r * FT + f, :],
                                              xT[:, c * CH:(c + 1) * CH], start=True, stop=True)
                    mm.then_inc(ms_act.sem, ms_act.up())
                pe.wait_ge(ms_free.sem, ms_free.seen(1))
                for i in range(TILES):
                    for f in range(FT):
                        mm = nc.tensor.matmul(ms3[:, i, :], hT[:, f, i * P:(i + 1) * P], wf[:, 2 * FT + f, :],
                                              start=(f == 0), stop=(f == FT - 1))
                    if i == TILES // 2 - 1:
                        mm.then_inc(ms_dve.sem, ms_dve.up())
                mm.then_inc(ms_dve.sem, ms_dve.up())
                pool_prep.count()
                pe.wait_ge(xn_ready.sem, xn_ready.next())
                transposed(lambda i: xn[:, i, :], TILES)
                pe.wait_ge(ms_free.sem, ms_free.next())
                for i in range(TILES):
                    mm = nc.tensor.matmul(ms3[:, i, :], xT[:, i * P:(i + 1) * P], at["wv1"],
                                          start=True, stop=True)
                mm.then_inc(ms_dve.sem, ms_dve.up())
                project1(0, 0, wide[1])
                project1(0, 1, wide[2])
                hi1_done.count(2)
                pe.wait_ge(ms_free.sem, ms_free.seen(1))
                pe.wait_ge(stack_done.sem, stack_done.next())
                for m in range(GH * TILES):
                    g, i = divmod(m, TILES)
                    if i == 0:
                        pe.wait_ge(stack_done.sem, stack_done.next())
                    if m >= 3:
                        pe.wait_ge(wide_free.sem, wide_free.next())
                    for c in range(2):
                        mm = nc.tensor.matmul(wide[m % 3][:, c * CH:(c + 1) * CH], ops1[:, 0, GH, i * P:(i + 1) * P],
                                              ops1[:, 0, g, c * CH:(c + 1) * CH], start=True, stop=True)
                    mm.then_inc(wide_full.sem, wide_full.up())
                pe.wait_ge(wide_free.sem, wide_free.next(3))
                maxima(GH * TILES)
                for n in range(GROUPS):
                    group(n)
                pe.wait_ge(av1_free.sem, av1_free.next())
                finish1()
                pe.wait_ge(ms_free.sem, ms_free.seen(1))
                transposed(lambda i: y[:, i, :], TILES)
                pe.wait_ge(ms_free.sem, ms_free.seen(1))
                for i in range(TILES):
                    mm = nc.tensor.matmul(ms3[:, i, :], xT[:, i * P:(i + 1) * P], at["wo1"],
                                          start=True, stop=True)
                mm.then_inc(ms_dve.sem, ms_dve.up())

            def token_x():
                pe.wait_ge(xn_ready.sem, xn_ready.next())
                transposed(lambda i: xn[:, i, :], B)

            def token_qkv(half):
                if half == 0:
                    pe.wait_ge(ms_free.sem, ms_free.next())
                else:
                    pe.wait_ge(ms_free.sem, ms_free.seen(1))
                for r in range(2):
                    s = 2 * half + r
                    mm = nc.tensor.matmul(ms[:, r * CH:r * CH + 3 * D], sT[:, s * P:(s + 1) * P],
                                          at["win"], start=True, stop=True)
                mm.then_inc(ms_dve.sem, ms_dve.up())

            def token_context():
                pe.wait_ge(tok_ready.sem, tok_ready.next())
                transposed(lambda i: y[:, i, :], B)

            def token_out():
                pe.wait_ge(ms_free.sem, ms_free.seen(1))
                for s in range(B):
                    mm = nc.tensor.matmul(ms3[:, s, :], cT[:, s * P:(s + 1) * P], at["wout"],
                                          start=True, stop=True)
                mm.then_inc(ms_dve.sem, ms_dve.up())

            def token_x1():
                pe.wait_ge(xn_ready.sem, xn_ready.next())
                transposed(lambda i: y[:, i, :], B)

            def token_gate():
                pe.wait_ge(ms_free.sem, ms_free.seen(1))
                for s in range(B):
                    mm = nc.tensor.matmul(ms[:, s * EXPERTS:(s + 1) * EXPERTS], xT[:, s * P:(s + 1) * P],
                                          at["wgate"], start=True, stop=True)
                mm.then_inc(ms_dve.sem, ms_dve.up())

            def combine_weights():
                pe.wait_ge(tok_ready.sem, tok_ready.next())
                pe.wait_ge(ms_free.sem, ms_free.next())
                for s in range(B):
                    mm = nc.tensor.transpose(ms[0:EXPERTS, s * P:(s + 1) * P], gt[7][:, s, :], at["ident"])
                mm.then_inc(ms_act.sem, ms_act.up())

            def second_biases():
                pe.wait_ge(ms_free.sem, ms_free.next())
                for s in range(B):
                    mm = nc.tensor.matmul(ms3[:, s, :], cbT[0:EXPERTS, s * P:(s + 1) * P],
                                          at["b2"][0:EXPERTS, :], start=True, stop=True)
                mm.then_inc(ms_dve.sem, ms_dve.up())

            def hidden(e):
                for f in range(4):
                    pe.wait_ge(relu_free.sem, relu_free.next())
                    nc.tensor.matmul(st[:, f // 2, f % 2 * CH:(f % 2 + 1) * CH],
                                     we[e][:, f * P:(f + 1) * P], x1T,
                                     start=True, stop=True).then_inc(h_full.sem, h_full.up())

            def expert_out(e):
                u = e % 2
                pe.wait_ge(relu_done.sem, relu_done.next(4))
                pe.wait_ge(y_free.sem, y_free.next())
                for s in range(B):
                    for f in range(4):
                        mm = nc.tensor.matmul(av[:, u * CH + s * D:u * CH + (s + 1) * D],
                                              relu[u][f][:, s * P:(s + 1) * P],
                                              we[e][:, HID + f * D:HID + (f + 1) * D],
                                              start=(f == 0), stop=(f == 3))
                mm.then_inc(y_full.sem, y_full.up())

            def chunk(following):
                combine_weights()
                hidden(0)
                second_biases()
                for e in range(EXPERTS):
                    if e < EXPERTS - 1:
                        hidden(e + 1)
                    if following and e == 2:
                        token_qkv(0)
                    if following and e == 5:
                        token_out()
                    if following and e == 7:
                        token_gate()
                    expert_out(e)
                    if following and e == 1:
                        token_x()
                    if following and e == 2:
                        token_qkv(1)
                    if following and e == 4:
                        token_context()
                    if following and e == 6:
                        token_x1()

            xn_ready.count()
            token_x()
            token_qkv(0)
            token_qkv(1)
            token_context()
            token_out()
            token_x1()
            token_gate()
            pe.wait_ge(sems["we_loaded"], EXPERTS * DMAS)
            apart(pe)
            with repeat(pe, "chunks", TILES - 1, every):
                chunk(True)
            chunk(False)

        @block.scalar
        def _(act):
            own = tally("act_own")
            ms_act, st_full, p_used = tally("ms_act"), tally("st_full"), tally("p_used")
            p_ready, av_full = signal("p_ready"), tally("av_full")
            rope_done, hi_done, rows_ready = tally("rope_done"), tally("hi_done"), tally("rows_ready")
            hi1_done, sg_ready, ms_free, av_free, av1_free = (
                signal("hi1_done"), signal("sg_ready"), signal("ms_free"), signal("av_free"), signal("av1_free"))
            sc_ready, ex_ready, h_full, relu_done = (
                tally("sc_ready"), signal("ex_ready"), tally("h_full"), signal("relu_done"))
            every = [own, ms_act, st_full, p_used, av_full, rope_done, hi_done, rows_ready,
                     sc_ready, h_full]
            act.sem_inc(sems["p_ready"], 2)
            act.sem_inc(sems["relu_done"], 4)

            act.sem_inc(sems["av_free"], 2)

            def copy(dst, src):
                return nc.scalar.activation(dst, src, ACT.Copy)

            def drain(dst, src):
                act.wait_ge(ms_act.sem, ms_act.next())
                copy(dst, src).then_inc(ms_free.sem, ms_free.up())

            def hi0(u, k, which):
                src = (qs, ks)[k]
                low, high = slice(0, 64), slice(64, P)
                moves = ([(low, low, QA, 0), (high, high, QA, 1), (low, low, QB, 0), (high, high, QB, 1)],
                         [(low, low, KA, 0), (high, low, KA, 0), (high, high, KA, 1), (low, high, KA, 1)])[k]
                for m in which:
                    to, frm, part, h = moves[m]
                    if m == 0:
                        act.wait_ge(rope_done.sem, rope_done.next(2))
                    copy(ops0[to, u, part, h, :], src[frm]).then_inc(hi_done.sem, hi_done.up())

            def values0(u):
                act.wait_ge(ms_act.sem, ms_act.next())
                copy(v0[:, u, :, 0, 0:C0], ms3[:, :, 0:C0])
                copy(v0[:, u, :, 1, C0:P], ms3[:, :, C0:P]).then_inc(ms_free.sem, ms_free.up())

            def exponentials0(kt):
                act.wait_ge(st_full.sem, st_full.next())
                if kt != 1:
                    act.wait_ge(p_used.sem, p_used.next())
                nc.scalar.activation(p0[:, kt % 2, kt * P:T], st[:, kt % 2, kt * P:T], ACT.Exp,
                                     scale=SCALE0).then_inc(p_ready.sem, p_ready.up())

            def drain_av(u, h, p, c):
                values, ones = (slice(0, 64), slice(64, P)) if h == 0 else (slice(64, P), slice(0, 64))
                cols = slice(c * CH, (c + 1) * CH)
                act.wait_ge(av_full.sem, av_full.next())
                copy(sums[values, u, cols], av[ones, cols])
                copy(outT[values, bass.ds(p, 1), cols].rearrange("r o t -> r (o t)"),
                     av[values, cols]).then_inc(av_free.sem, av_free.up())

            def minus_maxima(n):
                act.wait_ge(ms_act.sem, ms_act.next())
                nc.scalar.mul(mrows[0:n, :], ms[0:n, 0:P], -1.0).then_inc(rows_ready.sem, rows_ready.up())

            def pair(u, p, following):
                for s in range(2 * TILES):
                    h, kt = divmod(s, TILES)
                    exponentials0(kt)
                    if kt == TILES // 2:
                        drain_av(u, h, p, 0)
                    if s == TILES:
                        drain_av(u, 0, p, 1)
                    if following:
                        if s < 4:
                            hi0(1 - u, 0, [s])
                        if s == 6:
                            hi0(1 - u, 1, [0, 1])
                        if s == 7:
                            values0(1 - u)
                        if s == TILES:
                            hi0(1 - u, 1, [2, 3])
                drain_av(u, 1, p, 1)
                if following:
                    minus_maxima(2 * TILES)

            def biased(n, k, source=ms):
                act.wait_ge(ms_act.sem, ms_act.next())
                high_scale, whole_scale = at[("qc", "kc")[k]], at[("qb", "kb")[k]]
                nc.scalar.activation((xq, xk)[k], source[:], ACT.Identity, scale=whole_scale,
                                     bias=bias_whole[:, 2 * n + k:2 * n + k + 1])
                nc.scalar.activation((hq, hk)[k].bitcast(F32R), source[:], ACT.Identity, scale=high_scale,
                                     bias=bias_high[:, 2 * n + k:2 * n + k + 1]).then_inc(
                                         hi1_done.sem, hi1_done.up())

            def group(n):
                following = n < GROUPS - 1
                if following:
                    biased(n + 1, 0)
                    biased(n + 1, 1, wide[2])
                for s in range(GH * TILES):
                    kt, g = divmod(s, GH)
                    act.wait_ge(st_full.sem, st_full.next())
                    if g == 0 and kt != 1:
                        act.wait_ge(p_used.sem, p_used.next())
                    nc.scalar.activation(p1[:, kt % 2, g, :], st[:, g % 2, :], ACT.Exp,
                                         scale=SCALE1).then_inc(p_ready.sem, p_ready.up())
                    if n > 0 and s == 1:
                        values_out()
                if following:
                    minus_maxima(GH * TILES)

            def values_out():
                act.wait_ge(av_full.sem, av_full.next())
                copy(p0[:, 0, :], av[:]).then_inc(av1_free.sem, av1_free.up())

            act.wait_ge(sems["loaded"], 3 * DMAS)
            act.wait_ge(sems["prep_done"], 5)
            with repeat(act, "batch", B, every):
                drain(xT[:], ms[:])
                hi0(0, 0, range(4))
                values0(0)
                hi0(0, 1, range(4))
                minus_maxima(2 * TILES)
                with repeat(act, "pairs", PAIRS // 2 - 1, every) as j:
                    for u in range(2):
                        pair(u, 2 * j + u, True)
                pair(0, PAIRS - 2, True)
                pair(1, PAIRS - 1, False)
                drain(xT[:], ms[:])
                for k in range(2 * FT):
                    act.wait_ge(ms_act.sem, ms_act.next())
                    nc.scalar.activation(sg[k % 3], wide[k % 3][:, 0:CH], ACT.Silu).then_inc(
                        sg_ready.sem, sg_ready.up())
                drain(xT[:], ms[:])
                biased(0, 0, wide[1])
                biased(0, 1, wide[2])
                minus_maxima(GH * TILES)
                for n in range(GROUPS):
                    group(n)
                values_out()
                drain(xT[:], ms[:])

            def exponentials(dst, src, scale=1.0):
                act.wait_ge(sc_ready.sem, sc_ready.next())
                nc.scalar.activation(dst, src, ACT.Exp, scale=scale).then_inc(ex_ready.sem, ex_ready.up())

            def token_x1():
                act.wait_ge(ms_act.sem, ms_act.next())
                copy(x1T, ms[:, 0:CH])
                copy(xT[:, 0:CH], ms[:, 0:CH]).then_inc(ms_free.sem, ms_free.up())

            def rectified(e):
                for f in range(4):
                    act.wait_ge(h_full.sem, h_full.next())
                    nc.scalar.activation(relu[e % 2][f], st[:, f // 2, f % 2 * CH:(f % 2 + 1) * CH], ACT.Relu,
                                         bias=we[e][:, 2 * HID + f:2 * HID + f + 1]).then_inc(relu_done.sem,
                                                                                             relu_done.up())

            def chunk(following):
                drain(cbT[0:EXPERTS, :], ms[0:EXPERTS, 0:CH])
                for e in range(EXPERTS):
                    if following and e == 3:
                        drain(sT, ms[:, 0:CH])
                    if following and e == 5:
                        exponentials(ex, sc, SCALE2)
                    if following and e == 6:
                        drain(cT, ms[:, 0:CH])
                    rectified(e)
                if following:
                    token_x1()
                    exponentials(gt[1], gt[0])

            drain(sT, ms[:, 0:CH])
            exponentials(ex, sc, SCALE2)
            drain(cT, ms[:, 0:CH])
            token_x1()
            exponentials(gt[1], gt[0])
            with repeat(act, "chunks", TILES - 1, every):
                chunk(True)
            chunk(False)

        @block.gpsimd
        def _(pool):
            own, var_ready, rstd_ready = tally("pool_own"), tally("var_ready"), signal("rstd_ready")
            prep, outT_ready, hi_done, klo_done = (
                tally("pool_prep"), tally("outT_ready"), tally("hi_done"), tally("klo_done"))
            hi1_done, stack_done = tally("hi1_done"), tally("stack_done")
            every = [own, var_ready, prep, outT_ready, hi_done, klo_done, hi1_done, stack_done]
            low, high = slice(0, 64), slice(64, P)

            def inverse_roots():
                pool.wait_ge(var_ready.sem, var_ready.next())
                nc.gpsimd.tensor_tensor(rstd[:], var[:], neghalf[:].broadcast_to([P, TILES]), ALU.pow).then_inc(
                    rstd_ready.sem, rstd_ready.up())

            def klo(u):
                pool.wait_ge(hi_done.sem, hi_done.next(8))
                for h, rows in ((0, low), (1, high)):
                    nc.gpsimd.tensor_tensor(
                        ops0[rows, u, KB, h, :], ks[rows],
                        ops0[rows, u, KA, h, :].bitcast(F32), ALU.subtract).then_inc(klo_done.sem, klo_done.up())
                pool.wait_ge(klo_done.sem, klo_done.seen())
                apart(pool)

            def stack(u, k):
                pool.wait_ge(hi1_done.sem, hi1_done.next())
                x, h = (xq, xk)[k], (hq, hk)[k]
                if k == 0:
                    nc.gpsimd.tensor_tensor(ops1[:, u, GH, :], h, x, ALU.add).then_inc(stack_done.sem,
                                                                                       stack_done.up())
                else:
                    for g in range(GH):
                        r = slice(32 * g, 32 * g + 32)
                        nc.gpsimd.tensor_tensor(ops1[r, u, g, :], h[r], x[r], ALU.add).then_inc(
                            stack_done.sem, stack_done.up())
                pool.wait_ge(stack_done.sem, stack_done.seen())
                apart(pool)

            nc.gpsimd.memset(neghalf[:], -0.5).then_inc(own.sem, own.up())
            pool.wait_ge(own.sem, own.seen())
            pool.wait_ge(sems["loaded"], 3 * DMAS)
            inverse_roots()
            with repeat(pool, "batch", B, every) as b:
                pool.wait_ge(sems["batch_done"], b + 1)
                apart(pool)
                for u in range(2):
                    nc.gpsimd.memset(v0[:, u, :, 0, C0:P], 1.0).then_inc(own.sem, own.up())
                    nc.gpsimd.memset(v0[:, u, :, 1, 0:C0], 1.0).then_inc(own.sem, own.up())
                pool.wait_ge(own.sem, own.seen())
                apart(pool)
                for u in range(2):
                    for k in (QB, KB):
                        nc.gpsimd.memset(ops0[high, u, k, 0, :].bitcast(F32), 0.0).then_inc(own.sem, own.up())
                        nc.gpsimd.memset(ops0[low, u, k, 1, :].bitcast(F32), 0.0).then_inc(own.sem, own.up())
                pool.wait_ge(own.sem, own.seen())
                apart(pool)
                for u in range(2):
                    nc.gpsimd.memset(ops0[64:65, u, KB, 0, :].bitcast(F32), 1.0).then_inc(own.sem, own.up())
                    nc.gpsimd.memset(ops0[0:1, u, KB, 1, :].bitcast(F32), 1.0).then_inc(
                        (own, prep)[u].sem, (own, prep)[u].up())
                pool.wait_ge(prep.sem, prep.seen())
                apart(pool)
                klo(0)
                with repeat(pool, "pairs", PAIRS // 2 - 1, every):
                    klo(1)
                    klo(0)
                klo(1)
                inverse_roots()
                inverse_roots()
                pool.wait_ge(outT_ready.sem, outT_ready.next(2))
                apart(pool)
                nc.gpsimd.memset(parts[:, 0:10].bitcast(F32), 0.0).then_inc(own.sem, own.up())
                nc.gpsimd.memset(vals[:], 0.0).then_inc(own.sem, own.up())
                pool.wait_ge(own.sem, own.seen())
                apart(pool)
                nc.gpsimd.memset(v1[:, :, :, C1:C1 + 1], 1.0).then_inc(prep.sem, prep.up())
                inverse_roots()
                inverse_roots()
                for n in range(GROUPS):
                    stack(n % 2, 0)
                    stack(n % 2, 1)
                inverse_roots()
                inverse_roots()

            inverse_roots()
            inverse_roots()
            with repeat(pool, "chunks", TILES - 1, every):
                for _ in range(4):
                    inverse_roots()
            inverse_roots()
            inverse_roots()

        @block.vector
        def _(dve):
            own, ms_dve, ms_free = tally("dve_own"), tally("ms_dve"), signal("ms_free")
            x_loaded, var_ready, rstd_ready, xn_ready = (
                tally("x_loaded", step=DMAS), tally("var_ready"), tally("rstd_ready"), tally("xn_ready"))
            rope_done, hi_done, qlo_done = tally("rope_done"), tally("hi_done"), signal("qlo_done")
            av_free, outT_ready = tally("av_free", start=2), tally("outT_ready")
            wide_full, wide_free = tally("wide_full"), signal("wide_free")
            sg_ready, pool_prep, tok_ready = tally("sg_ready"), tally("pool_prep"), tally("tok_ready")
            sc_ready, ex_ready, batch_done = tally("sc_ready"), tally("ex_ready"), tally("batch_done")
            y_full, y_used, o_ready = tally("y_full"), tally("y_used", start=2), tally("o_ready")
            stored = tally("stored", step=DMAS)
            every = [own, ms_dve, x_loaded, var_ready, rstd_ready, xn_ready, hi_done,
                     av_free, wide_full, rope_done, outT_ready, sg_ready, pool_prep, tok_ready, sc_ready,
                     ex_ready, batch_done, y_full, y_used, o_ready, stored]
            low, high = slice(0, 64), slice(64, P)
            dve.sem_inc(sems["ms_free"], 1)
            dve.sem_inc(sems["batch_done"], 1)
            dve.sem_inc(sems["y_used"], 2)

            def tt(dst, a, b, op):
                return nc.vector.tensor_tensor(dst, a, b, op)

            def normalise(n, source, dst, done=None, meanwhile=None):
                for i in range(n):
                    last = nc.vector.bn_stats(stats[:, i, :], source(i))
                last.then_inc(own.sem, own.up())
                dve.wait_ge(own.sem, own.seen())
                apart(dve)
                for i in range(n):
                    last = nc.vector.bn_aggr(mv[:, i, :], stats[:, i, :])
                last.then_inc(own.sem, own.up())
                dve.wait_ge(own.sem, own.seen())
                nc.vector.tensor_scalar(var[:, 0:n], mv[:, 0:n, 1], EPS, None, ALU.add).then_inc(
                    var_ready.sem, var_ready.up())
                if meanwhile:
                    meanwhile()
                dve.wait_ge(rstd_ready.sem, rstd_ready.next())
                for i in range(n):
                    last = nc.vector.tensor_scalar(dst(i), source(i), mv[:, i, 0:1], rstd[:, i:i + 1],
                                                   ALU.subtract, ALU.mult)
                last.then_inc((done or own).sem, (done or own).up())
                if done is None:
                    dve.wait_ge(own.sem, own.seen())

            def add_normalised():
                for i in range(TILES):
                    if i % 4 == 0:
                        dve.wait_ge(ms_dve.sem, ms_dve.next())
                    last = nc.vector.bn_stats(stats[:, i, :], ms3[:, i, :])
                last.then_inc(own.sem, own.up())
                dve.wait_ge(own.sem, own.seen())
                apart(dve)
                for i in range(TILES):
                    last = nc.vector.bn_aggr(mv[:, i, :], stats[:, i, :])
                last.then_inc(own.sem, own.up())
                dve.wait_ge(own.sem, own.seen())
                nc.vector.tensor_scalar(var[:], mv[:, :, 1], EPS, None, ALU.add).then_inc(
                    var_ready.sem, var_ready.up())
                for i in range(TILES):
                    last = nc.vector.tensor_scalar(y[:, i, :], ms3[:, i, :], mv[:, i, 0:1], None, ALU.subtract)
                last.then_inc(own.sem, own.up())
                dve.wait_ge(own.sem, own.seen())
                dve.wait_ge(rstd_ready.sem, rstd_ready.next())
                for i in range(TILES):
                    last = nc.vector.scalar_tensor_tensor(out=xb[:, i, :], in0=y[:, i, :], scalar=rstd[:, i:i + 1],
                                                          in1=xb[:, i, :], op0=ALU.mult, op1=ALU.add)
                last.then_inc(own.sem, own.up())
                dve.wait_ge(own.sem, own.seen())

            def over(row, n):
                return row.unsqueeze(1).broadcast_to([P, n, D])

            def rope(k, c, source=ms):
                dve.wait_ge(ms_dve.sem, ms_dve.next())
                cols = slice(c * CH, (c + 1) * CH)
                tt(t1, source[:, 0:CH], cosT[:, cols], ALU.mult)
                tt(t2, source[:, CH:T], sinT[:, cols], ALU.mult).then_inc(own.sem, own.up())
                dve.wait_ge(own.sem, own.seen())
                tt((qs, ks)[k][:, cols], t1, t2, ALU.add).then_inc(rope_done.sem, rope_done.up())
                dve.wait_ge(rope_done.sem, rope_done.seen())

            def qlo(u):
                dve.wait_ge(hi_done.sem, hi_done.next(4))
                hi_done.count(4)
                for h, frm, to in ((0, low, high), (1, high, low)):
                    tt(ops0[to, u, QA, h, :], qs[frm], ops0[frm, u, QA, h, :].bitcast(F32),
                       ALU.subtract).then_inc(qlo_done.sem, qlo_done.up())

            def row_max(c, column, half, n, last=False):
                dve.wait_ge(ms_dve.sem, ms_dve.next())
                done = nc.vector.tensor_reduce(mx[:, c, column:column + 1], ms[:, half * CH:half * CH + n], AX.X,
                                               ALU.max)
                if last:
                    done.then_inc(own.sem, own.up())
                    dve.wait_ge(own.sem, own.seen())
                else:
                    done.then_inc(ms_free.sem, ms_free.up())

            def wide_max(m, column, n):
                dve.wait_ge(wide_full.sem, wide_full.next())
                nc.vector.tensor_reduce(mx[:, 0, column:column + 1], wide[m % 3][:, 0:n], AX.X,
                                        ALU.max).then_inc(wide_free.sem, wide_free.up())

            def maxima0():
                for m in range(2 * TILES):
                    h, i = tile0(m)
                    column = h * TILES + i
                    if i >= 4:
                        row_max(0, column, 0, CH)
                        row_max(1, column, 1, (i - 3) * P)
                    else:
                        row_max(0, column, (3 - i) % 2, (i + 1) * P, last=(m == 2 * TILES - 1))
                both = [mx[:, c, 0:2 * TILES].rearrange("p (h i) -> p h i", i=TILES)[:, :, 4:TILES] for c in range(2)]
                tt(both[0], both[0], both[1], ALU.max).then_inc(ms_free.sem, ms_free.up())

            def divide(u, p):
                dve.wait_ge(av_free.sem, av_free.next(4))
                nc.vector.reciprocal(sums[:, u], sums[:, u]).then_inc(own.sem, own.up())
                dve.wait_ge(own.sem, own.seen())
                o = outT[:, bass.ds(p, 1), :].rearrange("r o t -> r (o t)")
                return tt(o, o, sums[:, u], ALU.mult)

            def pair(u, p, following, further):
                if following:
                    rope(1, 0)
                    rope(1, 1)
                    qlo(1 - u)
                    maxima0()
                if further:
                    rope(0, 0)
                    rope(0, 1, av)
                if further:
                    divide(u, p).then_inc(own.sem, own.up())
                else:
                    divide(u, p).then_inc(outT_ready.sem, outT_ready.up())

            def finish1(n):
                dve.wait_ge(ms_dve.sem, ms_dve.next())
                o = ms3.rearrange("p i (g c) -> p i g c", g=GH)
                nc.vector.reciprocal(rinv, o[:, :, :, C1]).then_inc(own.sem, own.up())
                dve.wait_ge(own.sem, own.seen())
                tt(y[:, :, 32 * n:32 * n + 32].rearrange("p i (g c) -> p i g c", g=GH),
                   o[:, :, :, 0:C1], rinv.unsqueeze(3).broadcast_to([P, TILES, GH, C1]), ALU.mult).then_inc(
                       ms_free.sem, ms_free.up())

            def maxima1():
                for column in range(GH * TILES):
                    for c in range(2):
                        row_max(c, column, c, CH, last=(column == GH * TILES - 1 and c == 1))
                tt(mx[:, 0], mx[:, 0], mx[:, 1], ALU.max).then_inc(ms_free.sem, ms_free.up())

            dve.wait_ge(sems["loaded"], 3 * DMAS)
            nc.vector.tensor_copy(ident_r[:], at["ident"])
            nc.vector.tensor_copy(mask_st[:], at["mask_st"])
            nc.vector.tensor_copy(mask_qk[:], at["mask_qk"])
            nc.vector.tensor_scalar(wf[:].rearrange("p n d -> p (n d)"), wfi, 1.0 / 127.0, None,
                                    ALU.mult).then_inc(sems["prep_done"], 1)
            both = at["bias1"].rearrange("p (n k) -> p n k", k=2)
            for k in range(2):
                whole, high_part = (a.rearrange("p (n k) -> p n k", k=2)[:, :, k] for a in (bias_whole, bias_high[:]))
                nc.vector.tensor_scalar(whole, both[:, :, k], at[("qb", "kb")[k]], (0.0, at["ke"])[k], ALU.mult,
                                        ALU.add).then_inc(sems["prep_done"], 1)
                nc.vector.tensor_scalar(high_part, both[:, :, k], at[("qc", "kc")[k]], None,
                                        ALU.mult).then_inc(sems["prep_done"], 1)
            dve.wait_ge(sems["prep_done"], 5)
            dve.wait_ge(x_loaded.sem, x_loaded.next())
            normalise(TILES, lambda i: coming[:, i, :], lambda i: coming_norm[:, i, :], xn_ready)
            with repeat(dve, "batch", B, every) as b:
                dve.wait_ge(sems["batch_done"], b + 1)
                nc.vector.tensor_copy(xb[:], coming).then_inc(own.sem, own.up())
                rope(0, 0)
                rope(0, 1, wide[1])
                rope(1, 0, wide[2])
                rope(1, 1)
                qlo(0)
                for m in range(2 * TILES):
                    h, i = tile0(m)
                    wide_max(m, h * TILES + i, (i + 1) * P)
                rope(0, 0)
                rope(0, 1, av)
                apart(dve)
                with repeat(dve, "pairs", PAIRS // 2 - 1, every) as j:
                    for u in range(2):
                        pair(u, 2 * j + u, True, True)
                pair(0, PAIRS - 2, True, False)
                pair(1, PAIRS - 1, False, False)
                add_normalised()
                normalise(TILES, lambda i: xb[:, i, :], lambda i: xn[:, i, :], xn_ready)
                for k in range(2 * FT):
                    f, c = divmod(k, 2)
                    dve.wait_ge(sg_ready.sem, sg_ready.next())
                    tt(hT[:, f, c * CH:(c + 1) * CH], sg[k % 3], wide[k % 3][:, CH:T],
                       ALU.mult).then_inc(ms_free.sem, ms_free.up())
                add_normalised()
                normalise(TILES, lambda i: xb[:, i, :], lambda i: xn[:, i, :], xn_ready)
                dve.wait_ge(pool_prep.sem, pool_prep.next(2))
                dve.wait_ge(ms_dve.sem, ms_dve.next())
                tt(v1[:, :, :, 0:C1], ms3.rearrange("p i (h c) -> p i h c", h=H1),
                   over(at["bv1"], TILES).rearrange("p i (h c) -> p i h c", h=H1), ALU.add).then_inc(
                       ms_free.sem, ms_free.up())
                for m in range(GH * TILES):
                    wide_max(m, m, T)
                for n in range(GROUPS):
                    if n == GROUPS - 1:
                        dve.wait_ge(x_loaded.sem, x_loaded.next())
                        normalise(TILES, lambda i: coming[:, i, :], lambda i: coming_norm[:, i, :])
                    if n > 0:
                        finish1(n - 1)
                    if n < GROUPS - 1:
                        maxima1()
                finish1(GROUPS - 1)
                dve.wait_ge(ms_dve.sem, ms_dve.next())
                tt(y[:], ms3, over(at["bo1"], TILES), ALU.add).then_inc(own.sem, own.up())
                dve.wait_ge(own.sem, own.seen())
                tt(y[:], y[:], xn[:], ALU.add).then_inc(xn_ready.sem, xn_ready.up())
                dve.wait_ge(xn_ready.sem, xn_ready.seen())
                normalise(TILES, lambda i: y[:, i, :], lambda i: y[:, i, :])
                tt(x_all[:, bass.ds(b * TILES, TILES), :], xb[:], y[:], ALU.add).then_inc(
                    batch_done.sem, batch_done.up())
            dve.wait_ge(sems["batch_done"], B + 1)

            def total(dst, a, axis="p s t h -> p s h t", op=ALU.add):
                return nc.vector.tensor_reduce(dst, a.rearrange(axis), AX.X, op)

            def per_tile(a):
                return a.unsqueeze(2).broadcast_to([P, B, EXPERTS])

            def first_largest(p, dst):
                nc.vector.tensor_reduce(gm[2], p, AX.X, ALU.max).then_inc(own.sem, own.up())
                dve.wait_ge(own.sem, own.seen())
                tt(gt[2], p, per_tile(gm[2]), ALU.is_ge).then_inc(own.sem, own.up())
                dve.wait_ge(own.sem, own.seen())
                tt(gt[2], gt[2], at["rank"].unsqueeze(1).broadcast_to([P, B, EXPERTS]), ALU.mult).then_inc(
                    own.sem, own.up())
                dve.wait_ge(own.sem, own.seen())
                nc.vector.tensor_reduce(gm[3], gt[2], AX.X, ALU.max).then_inc(own.sem, own.up())
                dve.wait_ge(own.sem, own.seen())
                tt(dst, gt[2], per_tile(gm[3]), ALU.is_equal).then_inc(own.sem, own.up())
                dve.wait_ge(own.sem, own.seen())

            def token_norm(i, meanwhile=None):
                normalise(B, lambda s: x_all[:, bass.ds(s * TILES + i, 1), :].rearrange("p o d -> p (o d)"),
                          lambda s: xn[:, s, :], xn_ready, meanwhile)

            def token_qkv():
                for half in range(2):
                    dve.wait_ge(ms_dve.sem, ms_dve.next())
                    done = tt(qkv[:, 2 * half:2 * half + 2, :],
                              ms[:].rearrange("p (r c) -> p r c", r=2)[:, :, 0:3 * D],
                              at["bin"].unsqueeze(1).broadcast_to([P, 2, 3 * D]), ALU.add)
                    if half == 0:
                        done.then_inc(ms_free.sem, ms_free.up())
                    else:
                        done.then_inc(own.sem, own.up())
                        dve.wait_ge(own.sem, own.seen())

            def token_scores():
                for s in range(B):
                    last = tt(prod[:, s], qkv[:, s, 0:D].unsqueeze(1).broadcast_to([P, B, D]),
                              qkv[:, :, D:2 * D], ALU.mult)
                last.then_inc(own.sem, own.up())
                dve.wait_ge(own.sem, own.seen())
                nc.vector.tensor_reduce(sc.rearrange("p s t h -> p (s t h)"),
                                        flat.rearrange("p (n c) -> p n c", c=C1), AX.X, ALU.add).then_inc(
                                            own.sem, own.up())
                dve.wait_ge(own.sem, own.seen())
                total(m2, sc, op=ALU.max).then_inc(own.sem, own.up())
                dve.wait_ge(own.sem, own.seen())
                tt(sc, sc, m2.unsqueeze(2).broadcast_to([P, B, B, H1]), ALU.subtract).then_inc(
                    sc_ready.sem, sc_ready.up())

            def token_context():
                dve.wait_ge(ex_ready.sem, ex_ready.next())
                total(sm2, ex).then_inc(own.sem, own.up())
                dve.wait_ge(own.sem, own.seen())
                nc.vector.reciprocal(sm2, sm2).then_inc(own.sem, own.up())
                dve.wait_ge(own.sem, own.seen())
                tt(ex, ex, sm2.unsqueeze(2).broadcast_to([P, B, B, H1]), ALU.mult).then_inc(own.sem, own.up())
                dve.wait_ge(own.sem, own.seen())
                for s in range(B):
                    last = tt(prod[:, s].rearrange("p t (h c) -> p t h c", h=H1),
                              ex[:, s].unsqueeze(3).broadcast_to([P, B, H1, C1]),
                              qkv[:, :, 2 * D:3 * D].rearrange("p t (h c) -> p t h c", h=H1), ALU.mult)
                last.then_inc(own.sem, own.up())
                dve.wait_ge(own.sem, own.seen())
                total(y[:, 0:B, :], prod, "p s t e -> p s e t").then_inc(tok_ready.sem, tok_ready.up())

            def token_out(meanwhile=None):
                dve.wait_ge(ms_dve.sem, ms_dve.next())
                tt(y[:, 0:B, :], ms3[:, 0:B, :], over(at["bout"], B), ALU.add).then_inc(own.sem, own.up())
                dve.wait_ge(own.sem, own.seen())
                tt(y[:, 0:B, :], y[:, 0:B, :], xn[:, 0:B, :], ALU.add).then_inc(own.sem, own.up())
                dve.wait_ge(own.sem, own.seen())
                normalise(B, lambda s: y[:, s, :], lambda s: y[:, s, :], meanwhile=meanwhile)
                tt(y[:, 0:B, :], y[:, 0:B, :], over(at["ln1g"], B), ALU.mult).then_inc(own.sem, own.up())
                dve.wait_ge(own.sem, own.seen())
                tt(y[:, 0:B, :], y[:, 0:B, :], over(at["ln1b"], B), ALU.add).then_inc(xn_ready.sem, xn_ready.up())
                dve.wait_ge(xn_ready.sem, xn_ready.seen())
                nc.vector.tensor_copy(x1.rearrange("p (s d) -> p s d", s=B), y[:, 0:B, :]).then_inc(
                    own.sem, own.up())

            def token_gate(i):
                dve.wait_ge(ms_dve.sem, ms_dve.next())
                tt(gt[0], ms[:, 0:B * EXPERTS].rearrange("p (s e) -> p s e", s=B),
                   at["bgate"].unsqueeze(1).broadcast_to([P, B, EXPERTS]), ALU.add).then_inc(own.sem, own.up())
                dve.wait_ge(own.sem, own.seen())
                nc.vector.tensor_reduce(gm[0], gt[0], AX.X, ALU.max).then_inc(own.sem, own.up())
                dve.wait_ge(own.sem, own.seen())
                tt(gt[0], gt[0], per_tile(gm[0]), ALU.subtract).then_inc(sc_ready.sem, sc_ready.up())
                dve.wait_ge(ex_ready.sem, ex_ready.next())
                nc.vector.tensor_reduce(gm[1], gt[1], AX.X, ALU.add).then_inc(own.sem, own.up())
                dve.wait_ge(own.sem, own.seen())
                nc.vector.reciprocal(gm[1], gm[1]).then_inc(own.sem, own.up())
                dve.wait_ge(own.sem, own.seen())
                tt(gt[1], gt[1], per_tile(gm[1]), ALU.mult).then_inc(own.sem, own.up())
                dve.wait_ge(own.sem, own.seen())
                first_largest(gt[1], gt[3])
                nc.vector.scalar_tensor_tensor(out=gt[4], in0=gt[3], scalar=-2.0, in1=gt[1],
                                               op0=ALU.mult, op1=ALU.add).then_inc(own.sem, own.up())
                dve.wait_ge(own.sem, own.seen())
                first_largest(gt[4], gt[5])
                tt(gt[6], gt[3], gt[5], ALU.add).then_inc(own.sem, own.up())
                dve.wait_ge(own.sem, own.seen())
                tt(gt[6], gt[6], gt[1], ALU.mult).then_inc(own.sem, own.up())
                dve.wait_ge(own.sem, own.seen())
                nc.vector.tensor_reduce(gm[4], gt[6], AX.X, ALU.add).then_inc(own.sem, own.up())
                dve.wait_ge(own.sem, own.seen())
                nc.vector.reciprocal(gm[4], gm[4]).then_inc(own.sem, own.up())
                dve.wait_ge(own.sem, own.seen())
                tt(gt[7], gt[6], per_tile(gm[4]), ALU.mult).then_inc(tok_ready.sem, tok_ready.up())
                dve.wait_ge(tok_ready.sem, tok_ready.seen())
                nc.vector.tensor_copy(comb[:, bass.ds(i * B, B), :], gt[7]).then_inc(own.sem, own.up())

            combf = comb[:].rearrange("p n e -> p (n e)")

            def start_sum():
                dve.wait_ge(ms_dve.sem, ms_dve.next())
                return tt(acc, ms[:, 0:CH], x1, ALU.add)

            def add_expert(e, j):
                dve.wait_ge(y_full.sem, y_full.next())
                for s in range(B):
                    a = acc[:, s * D:(s + 1) * D]
                    last = nc.vector.scalar_tensor_tensor(
                        out=a, in0=av[:, e % 2 * CH + s * D:e % 2 * CH + (s + 1) * D],
                        scalar=combf[:, bass.ds((j * B + s) * EXPERTS + e, 1)],
                        in1=a, op0=ALU.mult, op1=ALU.add)
                last.then_inc(y_used.sem, y_used.up())
                dve.wait_ge(y_used.sem, y_used.seen())

            def finish(j):
                normalise(B, lambda s: acc[:, s * D:(s + 1) * D], lambda s: y[:, s, :])
                tt(y[:, 0:B, :], y[:, 0:B, :], over(at["ln2g"], B), ALU.mult).then_inc(own.sem, own.up())
                dve.wait_ge(own.sem, own.seen())
                tt(y[:, 0:B, :], y[:, 0:B, :], over(at["ln2b"], B), ALU.add).then_inc(own.sem, own.up())
                dve.wait_ge(own.sem, own.seen())
                normalise(B, lambda s: y[:, s, :], lambda s: y[:, s, :])
                dve.wait_ge(stored.sem, stored.next())
                tt(result.rearrange("p (s d) -> p s d", s=B), xs[:, :, bass.ds(j, 1), :].rearrange("p s o d -> p s (o d)"),
                   y[:, 0:B, :], ALU.add).then_inc(o_ready.sem, o_ready.up())
                dve.wait_ge(o_ready.sem, o_ready.seen())

            def chunk(j, following):
                if following:
                    token_norm(j + 1, lambda: start_sum().then_inc(ms_free.sem, ms_free.up()))
                    dve.wait_ge(xn_ready.sem, xn_ready.seen())
                else:
                    start_sum().then_inc(own.sem, own.up())
                    dve.wait_ge(own.sem, own.seen())
                add_expert(0, j)
                add_expert(1, j)
                if following:
                    token_qkv()
                    token_scores()
                add_expert(2, j)
                if following:
                    token_context()
                add_expert(3, j)
                if following:
                    token_out(lambda: add_expert(4, j))
                else:
                    add_expert(4, j)
                add_expert(5, j)
                add_expert(6, j)
                if following:
                    token_gate(j + 1)
                add_expert(7, j)
                finish(j)

            token_norm(0)
            token_qkv()
            token_scores()
            token_context()
            token_out()
            token_gate(0)
            with repeat(dve, "chunks", TILES - 1, every) as j:
                chunk(j, True)
            chunk(TILES - 1, False)


def kernel(**inputs):
    import numpy as np
    import concourse.bacc as bacc
    from concourse.bass_utils import run_bass_kernel_spmd

    f32 = np.float32
    g = {k: np.asarray(v) for k, v in inputs.items()}

    def row(v):
        return np.broadcast_to(v.reshape(1, -1), (P, v.size))

    x = g["L0_attn_x"]
    x_in = np.ascontiguousarray(np.concatenate([x, x[0:1]]).reshape((B + 1) * TILES, P, D).transpose(1, 0, 2)
                                .reshape(P, -1))
    swap = np.arange(P) // C0 * C0 + (np.arange(P) % C0 + C0 // 2) % C0
    wl0 = np.empty((PAIRS, P, 5, P), f32)
    for k, name in enumerate(("wq", "wk", "wv")):
        w = g[f"L0_attn_{name}"].reshape(PAIRS, P, D).transpose(0, 2, 1)
        wl0[:, :, 2 * k, :] = w
        if k < 2:
            wl0[:, :, 2 * k + 1, :] = w[:, :, swap]
    wl0 = wl0.reshape(PAIRS, P, WL0)
    inv = (1.0 / 10000.0 ** (np.arange(0, C0, 2, dtype=f32) / f32(C0))).astype(f32)
    angle = np.outer(np.arange(T, dtype=f32), inv).astype(f32).T[np.arange(P) % (C0 // 2)]
    sign = np.where(np.arange(P) % C0 < C0 // 2, -1.0, 1.0).astype(f32)[:, None]
    rope = np.concatenate([np.cos(angle), sign * np.sin(angle)], axis=1).astype(f32)
    wffn = np.concatenate([g["L0_ffn_w_gate"].T, g["L0_ffn_w_up"].T,
                           g["L0_ffn_w_down"].T.reshape(FT, P, D).transpose(1, 0, 2).reshape(P, -1)], axis=1)
    wmoe = np.concatenate([g["L1_ffn_w1"].transpose(0, 2, 1),
                           g["L1_ffn_w2"].transpose(0, 2, 1).reshape(EXPERTS, HID // P, P, D)
                           .transpose(0, 2, 1, 3).reshape(EXPERTS, P, -1),
                           g["L1_ffn_b1"].reshape(EXPERTS, HID // P, P).transpose(0, 2, 1)], axis=2)
    r = np.arange(P)
    dims = [(GH * n + r // 32) * C1 + r % C1 for n in range(GROUPS)]
    wqkv, bqkv = g["L1_attn_w_qkv"], g["L1_attn_b_qkv"]
    j = r % 32 // C1
    one = (r % 32 == 3 * C1)
    parts = {
        "wqk1": np.concatenate([wqkv[k * D + d].T for d in dims for k in range(2)], axis=1),
        "bias1": np.stack([bqkv[k * D + d] for d in dims for k in range(2)], axis=1),
        "qb": j == 2, "qc": 1.0 * (j < 2) - 1.0 * (j == 2),
        "kb": j == 1, "kc": 1.0 * ((j == 0) | (j == 2)) - 1.0 * (j == 1), "ke": one,
        "ident": np.eye(P), "mask_qk": np.where(r[:, None] >= r, 0.0, MASKED),
        "mask_st": np.where(r[:, None] <= r, 0.0, MASKED),
        "wo0": g["L0_attn_wo"].T.reshape(PAIRS, P, D).transpose(1, 0, 2).reshape(P, -1),
        "wv1": wqkv[2 * D:].T, "wo1": g["L1_attn_w_o"].T, "win": g["L1_ffn_in_proj_w"].T,
        "wout": g["L1_ffn_out_w"].T, "wgate": g["L1_ffn_gate_w"].T, "bv1": row(bqkv[2 * D:]),
        "bo1": row(g["L1_attn_b_o"]), "bin": row(g["L1_ffn_in_proj_b"]), "bout": row(g["L1_ffn_out_b"]),
        "bgate": row(g["L1_ffn_gate_b"]), "ln1g": row(g["L1_ffn_ln1_g"]), "ln1b": row(g["L1_ffn_ln1_b"]),
        "ln2g": row(g["L1_ffn_ln2_g"]), "ln2b": row(g["L1_ffn_ln2_b"]),
        "rank": row(np.arange(EXPERTS, 0, -1)), "b2": np.tile(g["L1_ffn_b2"], (P // EXPERTS, 1)),
    }
    pack = np.concatenate([np.asarray(parts[n], f32).reshape(P, w) for n, w in PACK], axis=1)
    arrays = {"x_in": x_in, "pack": pack, "rope": rope, "wl0": wl0, "wffn": wffn, "wmoe": wmoe}
    arrays = {n: np.ascontiguousarray(a) for n, a in arrays.items()}

    nc = bacc.Bacc("TRN2", target_bir_lowering=False, num_devices=1)
    aps = [nc.dram_tensor(n, a.shape, mybir.dt.from_np(a.dtype), kind="ExternalInput").ap()
           for n, a in arrays.items()]
    out = nc.dram_tensor("out", (TILES, P, B * D), F32, kind="ExternalOutput").ap()
    block_program(nc, *aps, out)
    result = run_bass_kernel_spmd(nc, [arrays], core_ids=[0]).results[0]["out"]
    return result.reshape(TILES, P, B, D).transpose(2, 0, 1, 3).reshape(B, T, D)
```
